# Optimizing a Trainium2 kernel written in Bass

```python
import numpy as np
import jax
import jax.numpy as jnp

def _softmax(x, axis=-1):
    return jax.nn.softmax(x, axis=axis)

def _gelu(x):
    return jax.nn.gelu(x, approximate=True)

def _silu(x):
    return jax.nn.silu(x)

def _sigmoid(x):
    return jax.nn.sigmoid(x)

def _layernorm(x, axis=-1, eps=1e-05):
    m = jnp.mean(x, axis=axis, keepdims=True)
    v = jnp.var(x, axis=axis, keepdims=True)
    return (x - m) / jnp.sqrt(v + eps)

def _scatter_add(tgt, idx, src, axis=0):
    return tgt.at[idx].add(src)

def _segment_sum(src, seg, n):
    return jax.ops.segment_sum(src, seg, n)
kernel_name = 'mk_gnn_ffn_d1_gnn_r8_90a7f8'

def setup_inputs(seed: int=0):
    np.random.seed(seed)
    _w = jnp.asarray

    def _rec_inputs():
        import jax
        import jax.numpy as jnp
        _gk = jax.random.key(seed)
        x = -0.0002117 + 1 * jax.random.normal(jax.random.fold_in(_gk, 1), (12500, 256), jnp.float32)
        _s = jax.random.randint(jax.random.fold_in(_gk, 2), (100000,), 0, 12500, jnp.int32)
        _d = jax.random.randint(jax.random.fold_in(_gk, 3), (100000,), 0, 12500, jnp.int32)
        _loop = jnp.arange(12500, dtype=jnp.int32)
        src = jnp.concatenate([_s, _d, _loop])
        dst = jnp.concatenate([_d, _s, _loop])
        _o = jnp.argsort(dst, stable=True)
        src = src[_o]
        dst = dst[_o]
        edge_weight = jax.random.uniform(jax.random.fold_in(_gk, 12), (212500,), jnp.float32, 0.0, 1)
        return (x, src, dst, edge_weight)
    x, src, dst, edge_weight = _rec_inputs()

    def _L0_gnn_setup():
        import jax, jax.numpy as jnp
        import numpy as np
        N_NODES = 12500
        N_EDGES = 400000
        IN_FEATS = 256
        OUT_FEATS = 256
        key = jax.random.key(seed)
        k1, k2, k3, k4, k5, k6 = jax.random.split(key, 6)
        features = jax.random.normal(k1, (N_NODES, IN_FEATS), dtype=jnp.float32)
        edge_src = jax.random.randint(k2, (N_EDGES,), 0, N_NODES, dtype=jnp.int64)
        edge_dst = jnp.sort(jax.random.randint(k3, (N_EDGES,), 0, N_NODES, dtype=jnp.int64))
        edge_weight = jax.random.uniform(k4, (N_EDGES,), dtype=jnp.float32)
        bound = 1.0 / np.sqrt(IN_FEATS)
        W = jax.random.uniform(k5, (OUT_FEATS, IN_FEATS), dtype=jnp.float32, minval=-bound, maxval=bound)
        b = jax.random.uniform(k6, (OUT_FEATS,), dtype=jnp.float32, minval=-bound, maxval=bound)
        return {'features': features, 'edge_src': edge_src, 'edge_dst': edge_dst, 'edge_weight': edge_weight, 'W': W, 'b': b}
    _L0_gnn_all = _L0_gnn_setup()
    _L0_gnn_in = {k: v for k, v in _L0_gnn_all.items() if k in ('W', 'b')}
    del _L0_gnn_all

    def _L0_ffn_setup():
        import jax, jax.numpy as jnp
        import numpy as np
        C = 256
        HID = 1024
        E = 8
        TEMP = 1.0
        key = jax.random.key(seed)
        ks = jax.random.split(key, 7)
        x = jax.random.normal(ks[0], (8, 2048, C), dtype=jnp.float32)
        W1 = jax.random.normal(ks[1], (C, HID), dtype=jnp.float32) * 0.02
        b1 = jnp.zeros((HID,), dtype=jnp.float32)
        Wg = jax.random.normal(ks[2], (HID, E), dtype=jnp.float32) * 0.02
        bg = jnp.zeros((E,), dtype=jnp.float32)
        Wd = jax.random.normal(ks[3], (E, HID, C), dtype=jnp.float32) * 0.02
        bd = jnp.zeros((E, C), dtype=jnp.float32)
        return {'x': x, 'W1': W1, 'b1': b1, 'Wg': Wg, 'bg': bg, 'Wd': Wd, 'bd': bd}
    _L0_ffn_all = _L0_ffn_setup()
    _L0_ffn_in = {k: v for k, v in _L0_ffn_all.items() if k in ('W1', 'b1', 'Wg', 'bg', 'Wd', 'bd')}
    del _L0_ffn_all
    return {'x': x, 'src': src, 'dst': dst, 'edge_weight': edge_weight, 'L0_gnn_W': _L0_gnn_in['W'], 'L0_gnn_b': _L0_gnn_in['b'], 'L0_ffn_W1': _L0_ffn_in['W1'], 'L0_ffn_b1': _L0_ffn_in['b1'], 'L0_ffn_Wg': _L0_ffn_in['Wg'], 'L0_ffn_bg': _L0_ffn_in['bg'], 'L0_ffn_Wd': _L0_ffn_in['Wd'], 'L0_ffn_bd': _L0_ffn_in['bd']}

def reference(x, src, dst, edge_weight, L0_gnn_W, L0_gnn_b, L0_ffn_W1, L0_ffn_b1, L0_ffn_Wg, L0_ffn_bg, L0_ffn_Wd, L0_ffn_bd):
    import jax
    import jax.numpy as jnp

    def _L0_gnn_ref(features, edge_src, edge_dst, edge_weight, W, b):
        import jax, jax.numpy as jnp
        import numpy as np
        N_NODES = 12500
        N_EDGES = 400000
        IN_FEATS = 256
        OUT_FEATS = 256
        msgs = features[edge_src] * edge_weight[:, None]
        agg = jax.ops.segment_sum(msgs, edge_dst, num_segments=N_NODES, indices_are_sorted=True)
        return jnp.einsum('ni,oi->no', agg, W) + b

    def _L0_ffn_ref(x, W1, b1, Wg, bg, Wd, bd):
        import jax, jax.numpy as jnp
        import numpy as np
        C = 256
        HID = 1024
        E = 8
        TEMP = 1.0
        orig_shape = x.shape
        xf = x.reshape(-1, orig_shape[-1])
        H = jax.nn.gelu(xf @ W1 + b1, approximate=False)
        probs = jax.nn.softmax((H @ Wg + bg) / TEMP, axis=-1)
        assign = jnp.argmax(probs, axis=-1)
        out = jnp.zeros_like(xf)
        for e in range(Wd.shape[0]):
            y = H @ Wd[e] + bd[e]
            sel = (assign == e)[:, None]
            out = out + jnp.where(sel, probs[:, e:e + 1] * y, 0.0)
        return out.reshape(orig_shape)
    x = x + _L0_gnn_ref(_layernorm(x, axis=-1), src, dst, edge_weight, L0_gnn_W, L0_gnn_b)
    x = x + _L0_ffn_ref(_layernorm(x, axis=-1)[None], L0_ffn_W1, L0_ffn_b1, L0_ffn_Wg, L0_ffn_bg, L0_ffn_Wd, L0_ffn_bd)[0]
    return x

_drawn_inputs = setup_inputs


def setup_inputs(seed=0):
    import zlib

    import numpy as np

    out = dict(_drawn_inputs(seed))
    spreads = {'L0_ffn_b1': (0.0, 0.8), 'L0_ffn_bg': (0.0, 0.667), 'L0_ffn_bd': (0.0, 0.8)}
    factors = {'L0_ffn_W1': 4.502, 'L0_ffn_Wg': 4.807, 'L0_ffn_Wd': 5.504}
    for name, (base, spread) in spreads.items():
        noise = np.random.default_rng([zlib.crc32(name.encode()), seed]).standard_normal(out[name].shape)
        drawn = base * np.exp(spread * noise) if base else spread * noise
        out[name] = jnp.asarray(drawn.astype(out[name].dtype))
    for name, factor in factors.items():
        out[name] = (out[name] * factor).astype(out[name].dtype)
    return out
```

```python
from contextlib import ExitStack

import concourse.bass as bass
from concourse import mybir

F32 = mybir.dt.float32
I32 = mybir.dt.int32
BF16 = mybir.dt.bfloat16
ALU = mybir.AluOpType
ACT = mybir.ActivationFunctionType
AX = mybir.AxisListType
DVE = mybir.EngineType.DVE
PE = mybir.EngineType.PE

P = 128
N = 12500
C = 256
KC = C // P
HID = 1024
HC = HID // P
E = 8
EPS = 1e-5

GROUP = 512
QB = GROUP // P
NF = -(-N // GROUP)
NODES = NF * GROUP
NB = NODES // P
EDGES = 212500
STEP_TILES = 16
NG = -(-EDGES // (P * STEP_TILES))
NG += NG % 2
TILES = NG * STEP_TILES
STEPS = NG + NF

SLOT = GROUP + P
NS = 1 << (2 + -(-STEP_TILES * P // GROUP) - 1).bit_length()
S_RING = 8
ROW = HID + C + E
LN_ROWS = 10
LN_CHUNKS = NB // LN_ROWS
NT = -(-(N + E * (P - 1)) // P)
NT = -(-NT // 3) * 3
RING2 = 3
IOTA = max(P, STEPS, NB, NT)
PAD_ROW = N + (-N) % 64


RSQRT_MAGIC = float(0x5F3759DF)
RSQRT_LINKS = 13
FFN_LINKS = 9 + RSQRT_LINKS


class Ticker:

    def __init__(self, eng, sem, base):
        self.eng, self.sem, self.base, self.n = eng, sem, base, 0

    def __call__(self, ins):
        self.n += 1
        ins.then_inc(self.sem, 1)
        self.eng.wait_ge(self.sem, self.base + self.n)


def build(nc, x, srcT, dstT, wT, gnn_WT, gnn_b, W1, b1T, Wg, bg, Wd, bd, out):
    assert PAD_ROW + P <= NODES and NB % LN_ROWS == 0
    ctx = ExitStack()
    with ctx:
        def sb(name, shape, dt=F32):
            return ctx.enter_context(nc.sbuf_tensor(name, shape, dt))

        def psum(name, shape=(P, 512), dt=F32):
            return ctx.enter_context(nc.psum_tensor(name, list(shape), dt))

        def sem(name):
            return ctx.enter_context(nc.semaphore(name))

        xn_dram = nc.dram_tensor("xn_table", (NODES, C), F32, kind="Internal").ap()
        row_dram = nc.dram_tensor("row_table", (NODES, ROW), F32, kind="Internal").ap()

        big = sb("big", [P, NB * C])
        ln_rows = big[:, :].rearrange("p (r c) -> p r c", c=C)
        xring = big[:, 0:2 * STEP_TILES * C].rearrange("p (t c) -> p t c", c=C)
        agg0 = 2 * STEP_TILES * C
        agg = big[:, agg0:agg0 + KC * NS * SLOT].rearrange("p (k n) -> p k n", k=KC)
        wd = big[:, 0:E * HC * C].rearrange("p (a c) -> p a c", c=C)
        after_wd = E * HC * C
        after_wd = max(after_wd, agg0 + KC * NS * SLOT)
        assert after_wd + 2 * QB * C + E * C <= NB * C
        xg, xn2 = (big[:, after_wd + a * QB * C:after_wd + (a + 1) * QB * C].rearrange("p (q c) -> p q c", c=C)
                   for a in range(2))
        bd_bc = big[:, after_wd + 2 * QB * C:after_wd + 2 * QB * C + E * C]

        src_i = sb("src_i", [P, TILES], I32)
        w_f = sb("w_f", [P, TILES])
        rel_f = sb("rel_f", [P, TILES])
        off_i = sb("off_i", [1, TILES], I32)
        steps_i = sb("steps_i", [P, STEPS, 8], I32)
        stage = sb("stage", [P, 2, STEP_TILES], I32)
        sel = sb("sel", [P, S_RING, P])

        wt = sb("wt", [P, KC, C])
        w1 = sb("w1", [P, KC, HID])
        b1 = sb("b1", [P, HC])
        wg = sb("wg", [P, HC, E])
        gnn_b_bc = sb("gnn_b_bc", [P, C])
        bg_bc = sb("bg_bc", [P, E])

        zero_col = sb("zero_col", [P, KC])
        ident = sb("ident", [P, P])
        ones = sb("ones", [P, P])
        upper = sb("upper", [P, P])
        iota_i = sb("iota_i", [P, IOTA], I32)
        iota = sb("iota", [P, IOTA])
        part_i = sb("part_i", [P, 1], I32)
        part = sb("part", [P, 1])

        hidT = sb("hidT", [P, HC, GROUP])
        rows = sb("rows", [P, QB, ROW])
        aggs = sb("aggs", [P, KC, GROUP])
        xn2T = sb("xn2T", [P, KC, GROUP])
        stats = sb("stats", [P, LN_ROWS, 6])
        meanvar = sb("meanvar", [P, NB, 2])
        rstd = sb("rstd", [P, NB])
        nhalf = sb("nhalf", [P, LN_ROWS])
        newton = sb("newton", [P, LN_ROWS])
        nmr = sb("nmr", [P, NB])
        logits = sb("logits", [P, NB, E])
        perm_i = sb("perm_i", [P, NT], I32)
        texp_i = sb("texp_i", [P, NT, 2], I32)

        scr = hidT[:, :, :].rearrange("p a b -> p (a b)")
        scr2 = rows[:, :, :].rearrange("p a b -> p (a b)")
        dst_i = scr[:, 0:TILES].bitcast(I32)
        base_i = scr[:, TILES:2 * TILES].bitcast(I32)
        base_f = scr2[:, 0:TILES]
        rem_i = scr2[0:1, TILES:2 * TILES].bitcast(I32)
        slot_i = scr2[0:1, 2 * TILES:3 * TILES].bitcast(I32)
        slot_f = scr2[:, 2 * TILES:3 * TILES]
        selv = sel[:, :, :].rearrange("p a b -> p (a b)")
        step_masks = selv[:, 0:2 * STEPS]
        u = [selv[:, a * STEPS:(a + 1) * STEPS] for a in range(7)]
        onehot = scr[:, 0:E * NB].rearrange("p (e b) -> p e b", e=E)
        score = scr[:, E * NB:2 * E * NB].rearrange("p (b e) -> p b e", e=E)
        incl = scr[:, 2 * E * NB:3 * E * NB].rearrange("p (e b) -> p e b", e=E)
        total = scr[:, 3 * E * NB:4 * E * NB].rearrange("p (e b) -> p e b", e=E)
        where = scr[:, 4 * E * NB:5 * E * NB].rearrange("p (e b) -> p e b", e=E)
        small = xn2T[:, :, :].rearrange("p a b -> p (a b)")
        best, valid, pos, slot_of, tile_of, tmp_b = (small[:, a * P:a * P + NB] for a in range(6))
        e_rank, e_cnt, e_mod, e_pad, e_cum, e_start = (small[:, 6 * P + a * E:6 * P + (a + 1) * E] for a in range(6))
        part1 = small[:, 7 * P:7 * P + 1]
        halves = aggs[:, :, :].rearrange("p a b -> p (a b)").bitcast(BF16)
        slot_oh = [halves[:, j * P:(j + 1) * P] for j in range(4)]
        tile_oh = [halves[:, 4 * P + j * 2 * NT:4 * P + (j + 1) * 2 * NT] for j in range(4)]
        zero = halves[:, 4 * P + 8 * NT:5 * P + 8 * NT]

        psA = [psum("psA0"), psum("psA1")]
        psH = [psum("psH0"), psum("psH1")]
        psE = [psum("psE0"), psum("psE1")]
        psG = psum("psG")
        psR = psum("psR")

        s_ln_load = [sem(f"ln_load{c}") for c in range(LN_CHUNKS)]
        s_ln_stat = sem("ln_stat")
        s_ln_coef = sem("ln_coef")
        s_ln_applied = sem("ln_applied")
        s_xn_stored = sem("xn_stored")
        s_edges = sem("edges_loaded")
        s_consts = sem("consts_loaded")
        s_small = sem("small_loaded")
        s_pool_c = sem("pool_consts")
        s_tab = sem("tables_dve")
        s_masks = sem("step_masks_ready")
        s_tabs = sem("tables_ready")
        s_onehot = sem("expert_onehot_ready")
        s_pos = sem("positions_ready")
        s_cnt_mm = sem("count_matmul")
        s_ring_free = sem("ring_half_free")
        s_staged = sem("staged")
        s_pass = sem("pool_waits_passed")
        s_pass_dve = sem("dve_waits_passed")
        s_gath = [sem("gathered0"), sem("gathered1")]
        s_sel = sem("sel_ready")
        s_edge_mm = sem("edge_matmul_done")
        s_acc = sem("accumulated")

        s_aggs = sem("aggs_ready")
        s_ffn = sem("ffn_dve")
        s_z = sem("z_done")
        s_xg = sem("xg_loaded")
        s_xg_free = sem("xg_free")
        s_xn2 = sem("xn2_ready")
        s_xt = sem("xn2T_transposed")
        s_xtc = sem("xn2T_copied")
        s_h = sem("hidden_matmul_done")
        s_gelu = sem("gelu_done")
        s_tr = sem("hidden_transposed")
        s_ev = sem("hidden_row_copied")
        s_g = sem("gate_done")
        s_rows = sem("rows_ready")
        s_rows_free = sem("rows_free")
        s_rows_st = sem("rows_stored")

        s_main = sem("main_done")
        s_wd = sem("wd_loaded")
        s_bd = sem("bd_loaded")
        s_rt = sem("route_dve")
        s_rank = sem("rank_matmul")
        s_oh = sem("perm_onehots")
        s_pm = sem("perm_matmul")
        s_perm = sem("perm_ready")

        s_r2free = sem("routed_row_free")
        s_st2 = sem("routed_staged")
        s_g2 = [sem(f"routed_gathered{i}") for i in range(RING2)]
        s_t2 = sem("routed_transposed")
        s_c2 = sem("routed_copied")
        s_y2 = sem("routed_product")
        s_o2 = sem("routed_out_ready")
        s_n2 = sem("routed_negmax")
        s_e2 = sem("routed_expsum")
        s_d2 = sem("routed_prob")
        s_tl = sem("routed_product_read")
        s_st = [sem(f"routed_stored{i}") for i in range(RING2)]

        grow = [rows[:, i, :] for i in range(RING2)]
        hT2 = [hidT[:, i * 2:i * 2 + 2, :].rearrange("p a b -> p (a b)").rearrange("p (c s) -> p c s", c=HC)
               for i in range(RING2)]
        ybuf = [xg[:, i, :] for i in range(RING2)]
        tbuf = [xn2[:, i, :] for i in range(RING2)]
        st_in = stage[:, 0, 0:RING2]
        st_out = sb("st_out", [P, RING2], I32)
        negmax = sb("negmax", [P, RING2])
        expv = sb("expv", [P, RING2, E])
        esum = sb("esum", [P, RING2])
        prob = sb("prob", [P, RING2])
        psT2 = [psA, psH, psE]
        psY2 = [psG[:, 0:C], psR[:, 0:C], psG[:, C:2 * C]]

        block = ctx.enter_context(nc.Block())

        @block.sync
        def _(sp):
            xr = x.rearrange("(p r) c -> p r c", p=P)
            for c in range(LN_CHUNKS):
                sp.dma_start(ln_rows[:, c * LN_ROWS:(c + 1) * LN_ROWS, :],
                             xr[:, c * LN_ROWS:(c + 1) * LN_ROWS, :]).then_inc(s_ln_load[c], 16)
                if c == 0:
                    sp.dma_start(dst_i, dstT[:, :]).then_inc(s_edges, 16)
                    sp.dma_start(base_i, dstT[0, :].partition_broadcast(P)).then_inc(s_edges, 16)
            sp.dma_start(w_f[:, :], wT[:, :]).then_inc(s_consts, 16)
            sp.dma_start(src_i[:, :], srcT[:, :]).then_inc(s_consts, 16)
            sp.dma_start(wt[:, :, :], gnn_WT.rearrange("(k p) o -> p k o", p=P)).then_inc(s_consts, 16)
            sp.dma_start(w1[:, :, :], W1.rearrange("(k p) h -> p k h", p=P)).then_inc(s_consts, 16)
            sp.dma_start(wg[:, :, :], Wg.rearrange("(c p) e -> p c e", p=P)).then_inc(s_consts, 16)
            sp.dma_start(b1[:, :], b1T[:, :]).then_inc(s_consts, 16)
            sp.dma_start(gnn_b_bc[:, :], gnn_b.partition_broadcast(P)).then_inc(s_consts, 16)
            sp.dma_start(bg_bc[:, :], bg.partition_broadcast(P)).then_inc(s_consts, 16)
            sp.wait_ge(s_consts, 16 * 8)
            sp.sem_inc(s_small, 1)
            sp.sem_inc(s_rows_free, 1)
            sp.wait_ge(s_xn_stored, 16 * LN_CHUNKS)
            sp.dma_start(xg[:, :, :], x[0:GROUP, :].rearrange("(q p) c -> p q c", p=P)).then_inc(s_xg, 16)

            def store_rows(f):
                sp.wait_ge(s_rows, f + 1)
                sp.dma_start(row_dram[bass.ds(f * GROUP, GROUP), :].rearrange("(q p) c -> p q c", p=P),
                             rows[:, :, :]).then_inc(s_rows_st, 16)
                sp.wait_ge(s_rows_st, f * 16 + 16)
                sp.sem_inc(s_rows_free, 1)

            with sp.Fori(0, NF - 1) as f:
                sp.wait_ge(s_xg_free, f + 1)
                sp.dma_start(xg[:, :, :], x[bass.ds(f * GROUP + GROUP, GROUP), :]
                             .rearrange("(q p) c -> p q c", p=P)).then_inc(s_xg, 16)
                store_rows(f)
            store_rows(NF - 1)
            sp.wait_ge(s_main, 1)
            for e in range(E):
                sp.dma_start(wd[:, e * HC:(e + 1) * HC, :],
                             Wd[e].rearrange("(c p) o -> p c o", p=P)).then_inc(s_wd, 16)
            sp.dma_start(bd_bc, bd.rearrange("e c -> (e c)").partition_broadcast(P)).then_inc(s_bd, 16)

        @block.gpsimd
        def _(pool):
            nc.gpsimd.memset(ones[:, :], 1.0).then_inc(s_pool_c, 1)
            nc.gpsimd.iota(iota_i[:, :], [[1, IOTA]], base=0, channel_multiplier=0).then_inc(s_pool_c, 1)
            nc.gpsimd.iota(part_i[:, :], [[0, 1]], base=0, channel_multiplier=1).then_inc(s_pool_c, 1)
            pool.wait_ge(s_pool_c, 3)
            nc.gpsimd.affine_select(out=ident[:, :], in_=ones[:, :], compare_op=ALU.is_equal, fill=0.0,
                                    base=0, pattern=[[-1, P]], channel_multiplier=1).then_inc(s_pool_c, 1)
            nc.gpsimd.affine_select(out=upper[:, :], in_=ones[:, :], compare_op=ALU.is_gt, fill=0.0,
                                    base=0, pattern=[[1, P]], channel_multiplier=-1).then_inc(s_pool_c, 1)
            pool.wait_ge(s_small, 1)
            pool.wait_ge(s_xn_stored, 16 * LN_CHUNKS)
            pool.wait_ge(s_acc, 2)
            with pool.Fori(0, NG // 2) as i:
                for h in range(2):
                    pool.wait_ge(s_ring_free, i * 2 + h + 1)
                    pool.sem_inc(s_pass, 1)
                    nc.gpsimd.tensor_copy(stage[:, h, :],
                                          src_i[:, bass.ds(i * 2 * STEP_TILES + h * STEP_TILES, STEP_TILES)]
                                          ).then_inc(s_staged, 1)
                    pool.wait_ge(s_staged, i * 2 + h + 1)
                    pool.sem_inc(s_pass, 1)
                    for j in range(STEP_TILES):
                        nc.gpsimd.indirect_dma_start(
                            out=xring[:, h * STEP_TILES + j, :], out_offset=None, in_=xn_dram[:, :],
                            in_offset=bass.IndirectOffsetOnAxis(ap=stage[:, h, j:j + 1], axis=0)
                        ).then_inc(s_gath[h], 16)

            def gather_routed(t, i):
                pool.wait_ge(s_r2free, t + 1)
                pool.sem_inc(s_pass, 1)
                nc.gpsimd.tensor_copy(st_in[:, i:i + 1], perm_i[:, bass.ds(t, 1)]).then_inc(s_st2, 1)
                pool.wait_ge(s_st2, t + 1)
                pool.sem_inc(s_pass, 1)
                nc.gpsimd.indirect_dma_start(
                    out=grow[i], out_offset=None, in_=row_dram[:, :],
                    in_offset=bass.IndirectOffsetOnAxis(ap=st_in[:, i:i + 1], axis=0)).then_inc(s_g2[i], 16)

            def scatter_routed(t, i):
                pool.wait_ge(s_o2, t + 1)
                pool.sem_inc(s_pass, 1)
                nc.gpsimd.indirect_dma_start(
                    out=out[:, :], out_offset=bass.IndirectOffsetOnAxis(ap=st_out[:, i:i + 1], axis=0),
                    in_=ybuf[i], in_offset=None, bounds_check=N - 1, oob_is_err=False).then_inc(s_st[i], 16)

            pool.wait_ge(s_perm, 1)
            pool.wait_ge(s_rows_free, NF + 1)
            for i in range(RING2):
                gather_routed(i, i)
            with pool.Fori(0, NT // RING2 - 1) as t3:
                for i in range(RING2):
                    scatter_routed(t3 * RING2 + i, i)
                    gather_routed(t3 * RING2 + RING2 + i, i)
            for i in range(RING2):
                scatter_routed(NT - RING2 + i, i)
            for i in range(RING2):
                pool.wait_ge(s_st[i], 16 * (NT // RING2))

        @block.scalar
        def _(act):
            xnr = xn_dram.rearrange("(p r) c -> p r c", p=P)
            for c in range(LN_CHUNKS):
                act.wait_ge(s_ln_coef, c + 1)
                with act.Fori(0, 2) as r2:
                    for j in range(LN_ROWS // 2):
                        r = bass.ds(r2 * (LN_ROWS // 2) + c * LN_ROWS + j, 1)
                        nc.scalar.activation(ln_rows[:, r, :], ln_rows[:, r, :], ACT.Identity, bias=nmr[:, r],
                                             scale=rstd[:, r]).then_inc(s_ln_applied, 1)
                act.wait_ge(s_ln_applied, (c + 1) * LN_ROWS)
                act.dma_start(xnr[:, c * LN_ROWS:(c + 1) * LN_ROWS, :],
                              ln_rows[:, c * LN_ROWS:(c + 1) * LN_ROWS, :]).then_inc(s_xn_stored, 16)
            act.wait_ge(s_small, 1)
            with act.Fori(0, NF) as f:
                for k in range(KC):
                    act.wait_ge(s_xt, f * KC + k + 1)
                    nc.scalar.activation(xn2T[:, k, :], psA[k][:, :], ACT.Copy).then_inc(s_xtc, 1)
                for c in range(HC):
                    act.wait_ge(s_h, f * HC + c + 1)
                    nc.scalar.activation(hidT[:, c, :], psH[c % 2][:, :], ACT.Gelu,
                                         bias=b1[:, c:c + 1]).then_inc(s_gelu, 1)
            with act.Fori(0, NT // RING2) as t3:
                for i in range(RING2):
                    act.wait_ge(s_n2, t3 * RING2 + i + 1)
                    nc.scalar.activation(expv[:, i, :], grow[i][:, HID + C:ROW], ACT.Exp,
                                         bias=negmax[:, i:i + 1], accum_out=esum[:, i:i + 1]).then_inc(s_e2, 1)
                    for k in range(2):
                        act.wait_ge(s_t2, t3 * (2 * RING2) + 2 * i + k + 1)
                        nc.scalar.activation(hT2[i][:, k * 4:k * 4 + 4, :],
                                             psT2[i][k][:, :].rearrange("p (c s) -> p c s", c=4),
                                             ACT.Copy).then_inc(s_c2, 1)

        @block.tensor
        def _(pe):
            pe.wait_ge(s_pool_c, 5)
            pe.wait_ge(s_masks, 1)
            nc.tensor.matmul(psG[:, 0:2 * STEPS], ones[:, :], step_masks,
                             start=True, stop=True).then_inc(s_cnt_mm, 1)
            pe.wait_ge(s_small, 1)
            pe.wait_ge(s_tabs, 1)
            pe.sem_inc(s_ring_free, 2)

            def gather_step(g, h):
                pe.wait_ge(s_gath[h], g * (8 * STEP_TILES) + (2 - h) * 8 * STEP_TILES)
                for j in range(STEP_TILES):
                    n = g * STEP_TILES + j
                    pe.wait_ge(s_sel, n + 1)
                    pe.wait_ge(s_acc, n + 1)
                    for k in range(KC):
                        mm = nc.tensor.matmul(psE[j % 2][:, k * P:(k + 1) * P],
                                              xring[:, h * STEP_TILES + j, k * P:(k + 1) * P],
                                              sel[:, j % S_RING, :], start=True, stop=True)
                    mm.then_inc(s_edge_mm, 1)
                pe.wait_ge(s_edge_mm, g * STEP_TILES + STEP_TILES)
                pe.sem_inc(s_ring_free, 1)

            def ffn_step(f):
                pe.wait_ge(s_aggs, f + 1)
                for q in range(QB):
                    for k in range(KC):
                        mm = nc.tensor.matmul(psA[q // 2][:, (q % 2) * C:(q % 2 + 1) * C],
                                              aggs[:, k, q * P:(q + 1) * P], wt[:, k, :],
                                              start=(k == 0), stop=(k == KC - 1))
                mm.then_inc(s_z, 1)
                pe.wait_ge(s_xn2, f + 1)
                for k in range(KC):
                    for q in range(QB):
                        mm = nc.tensor.transpose(psA[k][:, q * P:(q + 1) * P],
                                                 xn2[:, q, k * P:(k + 1) * P], ident[:, :])
                    mm.then_inc(s_xt, 1)
                pe.wait_ge(s_xtc, f * KC + KC)
                for c in range(HC):
                    if c >= 2:
                        pe.wait_ge(s_gelu, f * HC + c - 1)
                    for k in range(KC):
                        mm = nc.tensor.matmul(psH[c % 2][:, :], w1[:, k, c * P:(c + 1) * P], xn2T[:, k, :],
                                              start=(k == 0), stop=(k == KC - 1))
                    mm.then_inc(s_h, 1)
                for i in range(2 * QB):
                    half, q = i // QB, i % QB
                    if q == 0:
                        pe.wait_ge(s_gelu, f * HC + 4 * half + 4)
                    if i >= 2:
                        pe.wait_ge(s_ev, f * (2 * QB) + i - 1)
                    for j in range(4):
                        mm = nc.tensor.transpose(psA[i % 2][:, j * P:(j + 1) * P],
                                                 hidT[:, 4 * half + j, q * P:(q + 1) * P], ident[:, :])
                    mm.then_inc(s_tr, 1)
                for q in range(QB):
                    for c in range(HC):
                        mm = nc.tensor.matmul(psG[:, q * E:(q + 1) * E], hidT[:, c, q * P:(q + 1) * P],
                                              wg[:, c, :], start=(c == 0), stop=(c == HC - 1))
                mm.then_inc(s_g, 1)

            with pe.Fori(0, STEPS) as k:
                _, (kind, g, f) = nc.values_load_multi_w_load_instructions(
                    steps_i[0:1, bass.ds(k, 1), 0:3].rearrange("a b c -> a (b c)"), engines=(PE,),
                    min_val=0, max_val=NG)
                g, f = g.with_bounds(min_val=0, max_val=NG - 1), f.with_bounds(min_val=0, max_val=NF - 1)
                with pe.If(kind == 0):
                    gather_step(g, 0)
                with pe.If(kind == 1):
                    gather_step(g, 1)
                with pe.If(kind == 2):
                    ffn_step(f)

            pe.wait_ge(s_onehot, 1)
            oh = scr[:, 0:E * NB]
            for h in range(2):
                nc.tensor.matmul(psA[h][:, 0:4 * NB], upper[:, :], oh[:, h * 4 * NB:(h + 1) * 4 * NB],
                                 start=True, stop=True)
                mm = nc.tensor.matmul(psH[h][:, 0:4 * NB], ones[:, :], oh[:, h * 4 * NB:(h + 1) * 4 * NB],
                                      start=True, stop=True)
            mm.then_inc(s_rank, 1)
            pe.wait_ge(s_pos, 1)
            nc.tensor.matmul(psG[:, 0:2 * NT], zero, tile_oh[0], start=True, stop=False).then_inc(s_pm, 4)
            with pe.Fori(0, NB // 4) as b4:
                for j in range(4):
                    pe.wait_ge(s_oh, b4 * 4 + j + 1)
                    nc.tensor.matmul(psG[:, 0:2 * NT], slot_oh[j], tile_oh[j], start=False,
                                     stop=False).then_inc(s_pm, 1)
            nc.tensor.matmul(psG[:, 0:2 * NT], zero, tile_oh[0], start=False, stop=True).then_inc(s_pm, 1)

            def transposes(t3, i):
                pe.wait_ge(s_g2[i], t3 * 16 + 16)
                for k in range(2):
                    for j in range(4):
                        c = 4 * k + j
                        mm = nc.tensor.transpose(psT2[i][k][:, j * P:(j + 1) * P],
                                                 grow[i][:, c * P:(c + 1) * P], ident[:, :])
                    mm.then_inc(s_t2, 1)

            def product(t, i):
                e8 = pe.value_load(texp_i[0:1, bass.ds(t, 1), 0:1].rearrange("a b c -> a (b c)"),
                                   min_val=0, max_val=(E - 1) * HC)
                pe.wait_ge(s_c2, t * 2 + 2)
                pe.wait_ge(s_tl, t + 1)
                for c in range(HC):
                    mm = nc.tensor.matmul(psY2[i], hT2[i][:, c, :], wd[:, bass.ds(e8 + c, 1), :],
                                          start=(c == 0), stop=(c == HC - 1))
                mm.then_inc(s_y2, 1)

            pe.wait_ge(s_perm, 1)
            pe.wait_ge(s_wd, 16 * E)
            transposes(0, 0)
            with pe.Fori(0, NT // RING2 - 1) as t3:
                for i in range(RING2):
                    transposes(t3 + (i + 1) // RING2, (i + 1) % RING2)
                    product(t3 * RING2 + i, i)
            for i in range(RING2):
                if i < RING2 - 1:
                    transposes(NT // RING2 - 1, i + 1)
                product(NT - RING2 + i, i)

        @block.vector
        def _(dve):
            def moments(link, mv):
                n = mv.shape[1]
                diff, squares = nhalf[:, 0:n], newton[:, 0:n]
                nc.vector.tensor_tensor(mv[:, :, 0], stats[:, 0:n, 1], stats[:, 0:n, 4], ALU.add)
                nc.vector.tensor_tensor(squares, stats[:, 0:n, 2], stats[:, 0:n, 5], ALU.add)
                link(nc.vector.tensor_tensor(diff, stats[:, 0:n, 1], stats[:, 0:n, 4], ALU.subtract))
                nc.vector.tensor_scalar(mv[:, :, 0], mv[:, :, 0], 0.5, None, ALU.mult)
                link(nc.vector.scalar_tensor_tensor(out=diff, in0=diff, scalar=0.25, in1=diff,
                                                    op0=ALU.mult, op1=ALU.mult))
                link(nc.vector.scalar_tensor_tensor(out=mv[:, :, 1], in0=squares, scalar=1.0 / C, in1=diff,
                                                    op0=ALU.mult, op1=ALU.add))

            def rsqrt(link, y, var):
                n = y.shape[1]
                v, a = nhalf[:, 0:n], newton[:, 0:n]
                link(nc.vector.tensor_scalar(v, var, EPS, None, ALU.add))
                link(nc.vector.tensor_scalar(a.bitcast(I32), v.bitcast(I32), 1, None, ALU.logical_shift_right))
                link(nc.vector.tensor_scalar(y.bitcast(I32), a.bitcast(I32), -1.0, RSQRT_MAGIC, ALU.mult, ALU.add))
                link(nc.vector.tensor_scalar(v, v, -0.5, None, ALU.mult))
                for _ in range(3):
                    link(nc.vector.tensor_tensor(a, y, y, ALU.mult))
                    link(nc.vector.tensor_tensor(a, a, v, ALU.mult))
                    link(nc.vector.scalar_tensor_tensor(out=y, in0=a, scalar=1.5, in1=y, op0=ALU.add, op1=ALU.mult))

            tick = Ticker(dve, s_tab, 0)
            for c in range(LN_CHUNKS):
                dve.wait_ge(s_ln_load[c], 16)
                for j in range(LN_ROWS):
                    nc.vector.bn_stats(stats[:, j, :], ln_rows[:, c * LN_ROWS + j, :]).then_inc(s_ln_stat, 1)
                dve.wait_ge(s_ln_stat, (c + 1) * LN_ROWS)
                moments(tick, meanvar[:, c * LN_ROWS:(c + 1) * LN_ROWS, :])
                cs = slice(c * LN_ROWS, (c + 1) * LN_ROWS)
                rsqrt(tick, rstd[:, cs], meanvar[:, cs, 1])
                nc.vector.scalar_tensor_tensor(out=nmr[:, cs], in0=meanvar[:, cs, 0], scalar=-1.0,
                                               in1=rstd[:, cs], op0=ALU.mult, op1=ALU.mult).then_inc(s_ln_coef, 1)
            dve.wait_ge(s_pool_c, 5)
            dve.wait_ge(s_edges, 32)
            nc.vector.memset(zero_col[:, :], 0.0)
            nc.vector.tensor_copy(iota[:, :], iota_i[:, :])
            nc.vector.tensor_copy(part[:, :], part_i[:, :])
            nc.vector.tensor_tensor(rel_f[:, :], dst_i, base_i, ALU.subtract)
            tick(nc.vector.tensor_copy(base_f, base_i))
            tick(nc.vector.tensor_scalar(stats[:, 0, 0:1], part[:, :], float(GROUP), float(GROUP),
                                         ALU.mult, ALU.add))
            tick(nc.vector.tensor_scalar(slot_f, base_f, stats[:, 0, 0:1], 0.0, ALU.is_lt, ALU.add,
                                         accum_out=stats[:, 1, 0:1]))
            steps_of = stats[:, 2, 0:1].bitcast(I32)
            tick(nc.vector.tensor_scalar(steps_of, stats[:, 1, 0:1], float(STEP_TILES - 1), None, ALU.add))
            tick(nc.vector.tensor_scalar(steps_of, steps_of, STEP_TILES.bit_length() - 1, None,
                                         ALU.logical_shift_right))
            tick(nc.vector.tensor_tensor(stats[:, 4, 0:1], steps_of, part[:, :], ALU.add))
            nc.vector.tensor_scalar(step_masks[:, 0:STEPS], iota[:, 0:STEPS], stats[:, 4, 0:1], None, ALU.is_equal)
            nc.vector.tensor_scalar(step_masks[:, STEPS:2 * STEPS], iota[:, 0:STEPS], stats[:, 4, 0:1], None,
                                    ALU.is_gt).then_inc(s_masks, 1)
            log_group = GROUP.bit_length() - 1
            nc.vector.tensor_scalar(rem_i, base_i[0:1, :], GROUP - 1, None, ALU.bitwise_and)
            tick(nc.vector.tensor_scalar(slot_i, base_i[0:1, :], log_group, NS - 1, ALU.logical_shift_right,
                                         ALU.bitwise_and))
            tick(nc.vector.scalar_tensor_tensor(out=off_i[0:1, :], in0=slot_i, scalar=float(SLOT),
                                                in1=rem_i, op0=ALU.mult, op1=ALU.add))
            dve.wait_ge(s_cnt_mm, 1)
            nc.vector.tensor_copy(u[2].bitcast(I32), psG[:, 0:STEPS])
            tick(nc.vector.tensor_copy(u[3].bitcast(I32), psG[:, STEPS:2 * STEPS]))
            is_group, groups, gathers, odd, prev = (a.bitcast(I32) for a in (u[2], u[3], u[4], u[5], u[0]))
            nc.vector.tensor_scalar(prev, groups, float(NS - 1), None, ALU.add)
            tick(nc.vector.tensor_tensor(gathers, iota_i[:, 0:STEPS], groups, ALU.subtract))
            nc.vector.tensor_scalar(prev, prev, NS - 1, None, ALU.bitwise_and)
            nc.vector.tensor_scalar(u[6].bitcast(I32), groups, NS - 1, None, ALU.bitwise_and)
            tick(nc.vector.tensor_scalar(odd, gathers, 1, None, ALU.bitwise_and))
            nc.vector.scalar_tensor_tensor(out=steps_i[:, :, 0], in0=is_group, scalar=2.0, in1=odd,
                                           op0=ALU.mult, op1=ALU.max)
            nc.vector.tensor_scalar(steps_i[:, :, 1], gathers, float(NG - 1), None, ALU.min)
            nc.vector.tensor_copy(steps_i[:, :, 2], groups)
            nc.vector.tensor_scalar(steps_i[:, :, 3], u[6].bitcast(I32), float(SLOT), None, ALU.mult)
            tick(nc.vector.tensor_scalar(steps_i[:, :, 4], prev, float(SLOT), float(GROUP), ALU.mult, ALU.add))
            dve.wait_ge(s_xn_stored, 16 * LN_CHUNKS)
            dve.wait_ge(s_small, 1)
            nc.vector.memset(agg, 0.0).then_inc(s_acc, 2)
            dve.wait_ge(s_acc, 2)
            nc.vector.memset(stats[:, :, :], 0.0).then_inc(s_tabs, 1)

            def make_sel(g, j):
                col = g * STEP_TILES + j
                nc.vector.tensor_scalar(sel[:, j % S_RING, :], iota[:, 0:P], rel_f[:, bass.ds(col, 1)],
                                        w_f[:, bass.ds(col, 1)], ALU.is_equal, ALU.mult).then_inc(s_sel, 1)

            def gather_step(g):
                _, offs = nc.values_load_multi_w_load_instructions(
                    off_i[0:1, bass.ds(g * STEP_TILES, STEP_TILES)], engines=(DVE,),
                    min_val=0, max_val=(NS - 1) * SLOT + GROUP - 1,
                    skip_runtime_bounds_check_because="worked out modulo the ring's size")
                for j in range(4):
                    make_sel(g, j)
                for j in range(STEP_TILES):
                    if j + 4 < STEP_TILES:
                        make_sel(g, j + 4)
                    n = g * STEP_TILES + j
                    dve.wait_ge(s_edge_mm, n + 1)
                    dve.wait_ge(s_acc, n + 2)
                    win = agg[:, :, bass.ds(offs[j], P)]
                    nc.vector.tensor_tensor(win, psE[j % 2][:, 0:KC * P].rearrange("p (k n) -> p k n", k=KC),
                                            win, ALU.add).then_inc(s_acc, 1)
                dve.wait_ge(s_acc, g * STEP_TILES + STEP_TILES + 2)
                dve.sem_inc(s_pass_dve, 1)

            def ffn_step(f, slot, spill):
                link = Ticker(dve, s_ffn, f * FFN_LINKS)
                here, before = agg[:, :, bass.ds(slot, GROUP)], agg[:, :, bass.ds(spill, P)]
                link(nc.vector.tensor_copy(aggs[:, :, :], here))
                nc.vector.tensor_tensor(aggs[:, :, 0:P], aggs[:, :, 0:P], before, ALU.add).then_inc(s_aggs, 1)
                dve.wait_ge(s_aggs, f + 1)
                nc.vector.tensor_scalar(here, zero_col[:, :].unsqueeze(2).to_broadcast([P, KC, GROUP]), 0.0, None,
                                        ALU.add)
                link(nc.vector.tensor_scalar(before, zero_col[:, :].unsqueeze(2).to_broadcast([P, KC, P]), 0.0,
                                             None, ALU.add))
                dve.wait_ge(s_z, f + 1)
                dve.wait_ge(s_xg, f * 16 + 16)
                dve.wait_ge(s_rows_free, f + 1)
                x2 = rows[:, :, HID:HID + C]
                for a in range(2):
                    o = nc.vector.tensor_tensor(x2[:, 2 * a:2 * a + 2, :],
                                                psA[a][:, :].rearrange("p (q c) -> p q c", c=C),
                                                xg[:, 2 * a:2 * a + 2, :], ALU.add)
                link(o)
                dve.sem_inc(s_xg_free, 1)
                link(nc.vector.tensor_tensor(x2, x2, gnn_b_bc[:, :].unsqueeze(1).to_broadcast([P, QB, C]), ALU.add))
                for q in range(QB):
                    o = nc.vector.bn_stats(stats[:, q, :], x2[:, q, :])
                link(o)
                moments(link, meanvar[:, 0:QB, :])
                rsqrt(link, rstd[:, 0:QB], meanvar[:, 0:QB, 1])
                for q in range(QB):
                    o = nc.vector.tensor_scalar(xn2[:, q, :], x2[:, q, :], meanvar[:, q, 0:1],
                                                rstd[:, q:q + 1], ALU.subtract, ALU.mult)
                o.then_inc(s_xn2, 1)
                for i in range(2 * QB):
                    half, q = i // QB, i % QB
                    dve.wait_ge(s_tr, f * (2 * QB) + i + 1)
                    nc.vector.tensor_copy(rows[:, q, half * 512:(half + 1) * 512],
                                          psA[i % 2][:, :]).then_inc(s_ev, 1)
                dve.wait_ge(s_g, f + 1)
                lg = rows[:, :, HID + C:ROW]
                link(nc.vector.tensor_tensor(lg, psG[:, 0:QB * E].rearrange("p (q e) -> p q e", e=E),
                                             bg_bc[:, :].unsqueeze(1).to_broadcast([P, QB, E]), ALU.add))
                dve.wait_ge(s_ev, f * (2 * QB) + 2 * QB)
                nc.vector.tensor_copy(logits[:, bass.ds(f * QB, QB), :], lg).then_inc(s_rows, 1)
                assert link.n == FFN_LINKS, link.n

            with dve.Fori(0, STEPS) as k:
                _, (kind, g, f, slot, spill) = nc.values_load_multi_w_load_instructions(
                    steps_i[0:1, bass.ds(k, 1), 0:5].rearrange("a b c -> a (b c)"), engines=(DVE,),
                    min_val=0, max_val=NS * SLOT)
                g, f = g.with_bounds(min_val=0, max_val=NG - 1), f.with_bounds(min_val=0, max_val=NF - 1)
                slot = slot.with_bounds(min_val=0, max_val=(NS - 1) * SLOT)
                spill = spill.with_bounds(min_val=0, max_val=(NS - 1) * SLOT + GROUP)
                with dve.If(kind == 2):
                    ffn_step(f, slot, spill)
                with dve.If(kind <= 1):
                    gather_step(g)
            dve.wait_ge(s_acc, TILES + 2)
            dve.wait_ge(s_rows, NF)
            dve.wait_ge(s_gelu, NF * HC)
            dve.sem_inc(s_main, 1)

            route = Ticker(dve, s_rt, 0)
            nc.vector.memset(halves, 0.0)
            nc.vector.tensor_scalar(e_rank, iota[:, 0:E], -1.0, float(E), ALU.mult, ALU.add)
            nc.vector.tensor_scalar(tmp_b, iota[:, 0:NB], float(P), part[:, 0:1], ALU.mult, ALU.add)
            nc.vector.tensor_scalar(part1, part[:, :], 1.0, None, ALU.add)
            route(nc.vector.tensor_reduce(best, logits[:, :, :], AX.X, ALU.max))
            nc.vector.tensor_scalar(valid, tmp_b, float(N), None, ALU.is_lt)
            route(nc.vector.tensor_tensor(score, logits[:, :, :], best.unsqueeze(2).to_broadcast([P, NB, E]),
                                          ALU.is_equal))
            route(nc.vector.tensor_tensor(score, score, e_rank.unsqueeze(1).to_broadcast([P, NB, E]), ALU.mult))
            route(nc.vector.tensor_reduce(best, score, AX.X, ALU.max))
            route(nc.vector.tensor_copy(total, e_rank.unsqueeze(2).to_broadcast([P, E, NB])))
            route(nc.vector.tensor_tensor(onehot, total, best.unsqueeze(1).to_broadcast([P, E, NB]), ALU.is_equal))
            nc.vector.tensor_tensor(onehot, onehot, valid.unsqueeze(1).to_broadcast([P, E, NB]),
                                    ALU.mult).then_inc(s_onehot, 1)
            dve.wait_ge(s_rank, 1)
            for h in range(2):
                o = nc.vector.tensor_copy(scr[:, 3 * E * NB + h * 4 * NB:3 * E * NB + (h + 1) * 4 * NB],
                                          psH[h][:, 0:4 * NB])
            route(o)
            for e in range(E):
                o = nc.vector.tensor_tensor_scan(incl[:, e, :], ones[:, 0:NB], total[:, e, :], 0.0,
                                                 ALU.mult, ALU.add)
            route(o)
            e_int = e_mod.bitcast(I32)
            route(nc.vector.tensor_scalar(e_int, incl[:, :, NB - 1], float(P - 1), None, ALU.add))
            route(nc.vector.tensor_scalar(e_int, e_int, ~(P - 1) & 0xFFFF, None, ALU.bitwise_and))
            route(nc.vector.tensor_copy(e_pad, e_int))
            route(nc.vector.tensor_tensor_scan(e_cum, ones[:, 0:E], e_pad, 0.0, ALU.mult, ALU.add))
            nc.vector.tensor_tensor(e_start, e_cum, e_pad, ALU.subtract)
            route(nc.vector.tensor_tensor(where, incl, total, ALU.subtract))
            for h in range(2):
                part_h = scr[:, 4 * E * NB + h * 4 * NB:4 * E * NB + (h + 1) * 4 * NB]
                o = nc.vector.tensor_tensor(part_h, psA[h][:, 0:4 * NB], part_h, ALU.add)
            route(o)
            route(nc.vector.tensor_tensor(where, where, e_start.unsqueeze(2).to_broadcast([P, E, NB]), ALU.add))
            route(nc.vector.tensor_tensor(where, where, onehot, ALU.mult))
            nc.vector.tensor_scalar(tmp_b, valid, -float(2 * NT * P), float(2 * NT * P), ALU.mult, ALU.add)
            route(nc.vector.tensor_reduce(pos, where.rearrange("p e b -> p b e"), AX.X, ALU.add))
            pos_i, slot_ib, tile_ib = (a.bitcast(I32) for a in (best, valid, tmp_b))
            route(nc.vector.tensor_tensor(pos_i, pos, tmp_b, ALU.add))
            nc.vector.tensor_scalar(slot_ib, pos_i, P - 1, None, ALU.bitwise_and)
            route(nc.vector.tensor_scalar(tile_ib, pos_i, P.bit_length() - 1, None, ALU.logical_shift_right))
            nc.vector.tensor_copy(slot_of, slot_ib)
            nc.vector.tensor_copy(tile_of, tile_ib).then_inc(s_pos, 1)
            dve.wait_ge(s_pos, 1)
            with dve.Fori(0, NB // 4) as b4:
                for j in range(4):
                    b = b4 * 4 + j
                    dve.wait_ge(s_pm, b + 1)
                    nc.vector.tensor_scalar(slot_oh[j], iota[:, 0:P], slot_of[:, bass.ds(b, 1)], None, ALU.is_equal)
                    nc.vector.tensor_scalar(tile_oh[j][:, 0:NT], iota[:, 0:NT], tile_of[:, bass.ds(b, 1)],
                                            part1, ALU.is_equal, ALU.mult)
                    nc.vector.tensor_scalar(tile_oh[j][:, NT:2 * NT], iota[:, 0:NT], tile_of[:, bass.ds(b, 1)],
                                            iota[:, bass.ds(b, 1)], ALU.is_equal, ALU.mult).then_inc(s_oh, 1)
            tile0, owner = score.rearrange("p b e -> p (b e)")[:, 0:NT], total.rearrange("p e b -> p (e b)")[:, 0:NT]
            route(nc.vector.tensor_scalar(tile0, iota[:, 0:NT], float(P), None, ALU.mult))
            route(nc.vector.tensor_scalar(owner, tile0, e_start[:, 1:2], None, ALU.is_ge))
            for e in range(2, E):
                route(nc.vector.scalar_tensor_tensor(out=owner, in0=tile0, scalar=e_start[:, e:e + 1], in1=owner,
                                                     op0=ALU.is_ge, op1=ALU.add))
            nc.vector.tensor_scalar(texp_i[:, :, 0], owner, float(HC), None, ALU.mult)
            nc.vector.tensor_scalar(texp_i[:, :, 1], owner, float(C), None, ALU.mult)
            dve.wait_ge(s_pm, 4 + NB + 1)
            lane1, block = psG[:, 0:NT], psG[:, NT:2 * NT]
            empty, node = (where.rearrange("p e b -> p (e b)")[:, a * P:a * P + NT] for a in range(2))
            route(nc.vector.tensor_scalar(empty, lane1, 1.0, -1.0, ALU.min, ALU.mult))
            nc.vector.tensor_scalar(part1, part1, float(PAD_ROW), None, ALU.add)
            route(nc.vector.tensor_scalar(empty, empty, 1.0, None, ALU.add))
            route(nc.vector.scalar_tensor_tensor(out=node, in0=empty, scalar=part1, in1=lane1,
                                                 op0=ALU.mult, op1=ALU.add))
            route(nc.vector.scalar_tensor_tensor(out=node, in0=block, scalar=float(P), in1=node,
                                                 op0=ALU.mult, op1=ALU.add))
            nc.vector.tensor_scalar(perm_i[:, :], node, -1.0, None, ALU.add).then_inc(s_perm, 1)
            dve.wait_ge(s_perm, 1)

            dve.wait_ge(s_bd, 16)
            dve.sem_inc(s_r2free, RING2)
            dve.sem_inc(s_tl, 2)

            def routed_tile(t, t3, i, again):
                dve.wait_ge(s_g2[i], t3 * 16 + 16)
                nc.vector.tensor_reduce(negmax[:, i:i + 1], grow[i][:, HID + C:ROW], AX.X, ALU.max,
                                        negate=True).then_inc(s_n2, 1)
                dve.wait_ge(s_e2, t + 1)
                nc.vector.reciprocal(prob[:, i:i + 1], esum[:, i:i + 1]).then_inc(s_d2, 1)
                e256 = dve.value_load(texp_i[0:1, bass.ds(t, 1), 1:2].rearrange("a b c -> a (b c)"),
                                      min_val=0, max_val=(E - 1) * C)
                if again:
                    dve.wait_ge(s_st[i], t3 * 16)
                nc.vector.tensor_copy(st_out[:, i:i + 1], perm_i[:, bass.ds(t, 1)])
                dve.wait_ge(s_y2, t + 1)
                nc.vector.tensor_tensor(tbuf[i], psY2[i], bd_bc[:, bass.ds(e256, C)], ALU.add).then_inc(s_tl, 1)
                dve.wait_ge(s_tl, t + 3)
                dve.wait_ge(s_d2, t + 1)
                nc.vector.scalar_tensor_tensor(out=ybuf[i], in0=tbuf[i], scalar=prob[:, i:i + 1],
                                               in1=grow[i][:, HID:HID + C], op0=ALU.mult,
                                               op1=ALU.add).then_inc(s_o2, 1)
                dve.wait_ge(s_o2, t + 1)
                dve.sem_inc(s_r2free, 1)

            for i in range(RING2):
                routed_tile(i, 0, i, False)
            with dve.Fori(1, NT // RING2) as t3:
                for i in range(RING2):
                    routed_tile(t3 * RING2 + i, t3, i, True)


def kernel(**inputs):
    import numpy as np
    import concourse.bacc as bacc
    from concourse.bass_utils import run_bass_kernel_spmd as run

    def edges(name, fill):
        a = np.ascontiguousarray(inputs[name])
        full = np.full((TILES * P,), fill, a.dtype)
        full[:EDGES] = a
        return np.ascontiguousarray(full.reshape(TILES, P).T)

    x = np.zeros((NODES, C), np.float32)
    x[:N] = inputs["x"]
    arrays = {
        "x": x,
        "srcT": edges("src", 0),
        "dstT": edges("dst", N - 1),
        "wT": edges("edge_weight", 0),
        "gnn_WT": np.ascontiguousarray(np.asarray(inputs["L0_gnn_W"]).T),
        "gnn_b": np.ascontiguousarray(inputs["L0_gnn_b"]),
        "W1": np.ascontiguousarray(inputs["L0_ffn_W1"]),
        "b1T": np.ascontiguousarray(np.asarray(inputs["L0_ffn_b1"]).reshape(HC, P).T),
        "Wg": np.ascontiguousarray(inputs["L0_ffn_Wg"]),
        "bg": np.ascontiguousarray(inputs["L0_ffn_bg"]),
        "Wd": np.ascontiguousarray(inputs["L0_ffn_Wd"]),
        "bd": np.ascontiguousarray(inputs["L0_ffn_bd"]),
    }
    nc = bacc.Bacc("TRN2", target_bir_lowering=False, num_devices=1)
    feeds, args = {}, []
    for name, a in arrays.items():
        feeds[f"in_{name}"] = a
        args.append(nc.dram_tensor(f"in_{name}", a.shape, mybir.dt.from_np(a.dtype), kind="ExternalInput").ap())
    args.append(nc.dram_tensor("out_0", (N, C), F32, kind="ExternalOutput").ap())
    build(nc, *args)
    r = run(nc, [feeds], core_ids=[0])
    return r.results[0]["out_0"]
```

```python
from contextlib import ExitStack

import concourse.bass as bass
from concourse import mybir

F32 = mybir.dt.float32
I32 = mybir.dt.int32
ALU = mybir.AluOpType
ACT = mybir.ActivationFunctionType
AX = mybir.AxisListType
DVE = mybir.EngineType.DVE
PE = mybir.EngineType.PE

P = 128
N = 12500
C = 256
KC = C // P
HID = 1024
HC = HID // P
E = 8
EPS = 1e-5

GROUP = 512
QB = GROUP // P
NF = -(-N // GROUP)
NODES = NF * GROUP
NB = NODES // P
EDGES = 212500
STEP_TILES = 16
NG = -(-EDGES // (P * STEP_TILES))
SECTIONS = 3
NG += -NG % SECTIONS
QUAD = 4
QUADS = STEP_TILES // QUAD
NARROW = 64
LANES = 32
TILES = NG * STEP_TILES
TABLE = TILES + STEP_TILES
STEPS = NG + NF

SLOT = GROUP + P
NS = 1 << (2 + -(-STEP_TILES * P // GROUP) - 1).bit_length()
S_RING = 4
ACC0 = STEP_TILES
MM0 = SECTIONS * STEP_TILES
GATE_COLS = LANES
ROW = C + HID + E
LOGITS = C + HID
LN_ROWS = 10
LN_CHUNKS = NB // LN_ROWS
NT = (N + E * (P - 1)) // P
RING2 = 4
ROUNDS = NT // RING2
IOTA = max(P, STEPS, NB, NT)
PAD_ROW = N + (-N) % 64


RSQRT_MAGIC = float(0x5F3759DF)
RSQRT_LINKS = 13
FFN_LINKS = 8 + RSQRT_LINKS


class Ticker:

    def __init__(self, eng, sem, base):
        self.eng, self.sem, self.base, self.n = eng, sem, base, 0

    def __call__(self, ins):
        self.n += 1
        ins.then_inc(self.sem, 1)
        self.eng.wait_ge(self.sem, self.base + self.n)


def build(nc, x, srcT, dstT, wT, gnn_WT, gnn_b, W1, b1T, Wg, bg, Wd, bd, out):
    assert PAD_ROW + P <= NODES and NB % LN_ROWS == 0
    ctx = ExitStack()
    with ctx:
        def sb(name, shape, dt=F32):
            return ctx.enter_context(nc.sbuf_tensor(name, shape, dt))

        def psum(name, shape=(P, 512), dt=F32):
            return ctx.enter_context(nc.psum_tensor(name, list(shape), dt))

        def sem(name):
            return ctx.enter_context(nc.semaphore(name))

        xn_dram = nc.dram_tensor("xn_table", (NODES, C), F32, kind="Internal").ap()
        row_dram = nc.dram_tensor("row_table", (NODES, ROW), F32, kind="Internal").ap()

        big = sb("big", [P, NB * C])
        ln_rows = big[:, :].rearrange("p (r c) -> p r c", c=C)
        xring = big[:, 0:SECTIONS * STEP_TILES * C].rearrange("p (t c) -> p t c", c=C)
        agg0 = SECTIONS * STEP_TILES * C
        agg = big[:, agg0:agg0 + KC * NS * SLOT].rearrange("p (k n) -> p k n", k=KC)
        wd = big[:, 0:E * HC * C].rearrange("p (a c) -> p a c", c=C)
        after_wd = E * HC * C
        bd_bc = big[:, after_wd:after_wd + E * C]
        after_wd = max(after_wd + E * C, agg0 + KC * NS * SLOT)
        assert after_wd + 2 * QB * C + GROUP <= NB * C
        xg, xn2 = (big[:, after_wd + a * QB * C:after_wd + (a + 1) * QB * C].rearrange("p (q c) -> p q c", c=C)
                   for a in range(2))

        gate_parts = big[:, after_wd + 2 * QB * C:after_wd + 2 * QB * C + GROUP]

        src_i = sb("src_i", [P, TABLE], I32)
        w_f = sb("w_f", [P, TABLE])
        rel_f = sb("rel_f", [P, TABLE])
        shift_f = sb("shift_f", [P, TILES // QUAD])
        off_i = sb("off_i", [1, TILES], I32)
        quads_i = sb("quads_i", [1, NG, 2 + QUADS], I32)
        steps_i = sb("steps_i", [P, STEPS, 6], I32)
        stage = sb("stage", [P, SECTIONS, STEP_TILES], I32)
        parts = sb("parts", [P, 2, C])
        sel = parts[:, :, :].rearrange("p a b -> p (a b)").rearrange("p (s n) -> p s n", n=P)
        place = sb("place", [P, QUADS, NARROW])
        selv = sb("sel_narrow", [P, SECTIONS * STEP_TILES * LANES])

        wt = sb("wt", [P, KC, C])
        w1 = sb("w1", [P, KC, HID])
        b1 = sb("b1", [P, HC])
        wg = sb("wg", [P, HC, GATE_COLS])
        fold = sb("fold", [P, E])
        gnn_b_bc = sb("gnn_b_bc", [P, C])
        bg_bc = sb("bg_bc", [P, E])

        zero_col = sb("zero_col", [P, KC])
        ident = sb("ident", [P, P])
        ones = sb("ones", [P, P])
        upper = sb("upper", [P, P])
        iota_i = sb("iota_i", [P, IOTA], I32)
        iota = sb("iota", [P, IOTA])
        part_i = sb("part_i", [P, 1], I32)
        part = sb("part", [P, 1])

        hidT = sb("hidT", [P, HC, GROUP])
        rows = sb("rows", [P, QB, ROW])
        aggs = sb("aggs", [P, KC, GROUP])
        xn2T = sb("xn2T", [P, KC, GROUP])
        stats = sb("stats", [P, LN_ROWS, 6])
        meanvar = sb("meanvar", [P, NB, 2])
        rstd = sb("rstd", [P, NB])
        nhalf = sb("nhalf", [P, LN_ROWS])
        newton = sb("newton", [P, LN_ROWS])
        nmr = sb("nmr", [P, NB])
        logits = sb("logits", [P, NB, E])
        perm_i = rel_f[:, 0:NT].bitcast(I32)
        texp_i = rel_f[:, NT:3 * NT].bitcast(I32).rearrange("p (t a) -> p t a", a=2)

        scr = hidT[:, :, :].rearrange("p a b -> p (a b)")
        scr2 = rows[:, :, :].rearrange("p a b -> p (a b)")
        dst_i = scr[:, 0:TABLE].bitcast(I32)
        base_i = scr[:, TABLE:2 * TABLE].bitcast(I32)
        base_f = scr2[:, 0:TILES]
        rem_i = scr2[0:1, TILES:2 * TILES].bitcast(I32)
        slot_i = scr2[0:1, 2 * TILES:3 * TILES].bitcast(I32)
        slot_f = scr2[:, 2 * TILES:3 * TILES]
        sel_narrow = selv[:, :].rearrange("p (s n) -> p s n", n=LANES)
        step_masks = selv[:, 0:2 * STEPS + 2 * NG]
        span_tile, span_quad = (xn2T[:, a, 0:NG] for a in range(2))
        u = [selv[:, a * STEPS:(a + 1) * STEPS] for a in range(7)]
        onehot = scr[:, 0:E * NB].rearrange("p (e b) -> p e b", e=E)
        score = scr[:, E * NB:2 * E * NB].rearrange("p (b e) -> p b e", e=E)
        incl = scr[:, 2 * E * NB:3 * E * NB].rearrange("p (e b) -> p e b", e=E)
        total = scr[:, 3 * E * NB:4 * E * NB].rearrange("p (e b) -> p e b", e=E)
        where = scr[:, 4 * E * NB:5 * E * NB].rearrange("p (e b) -> p e b", e=E)
        small = xn2T[:, :, :].rearrange("p a b -> p (a b)")
        best, valid, pos, slot_of, tile_of, tmp_b = (small[:, a * P:a * P + NB] for a in range(6))
        e_rank, e_cnt, e_mod, e_pad, e_cum, e_start = (small[:, 6 * P + a * E:6 * P + (a + 1) * E] for a in range(6))
        part1 = small[:, 7 * P:7 * P + 1]
        onehots = aggs[:, :, :].rearrange("p a b -> p (a b)")
        slot_oh = [onehots[:, j * P:(j + 1) * P] for j in range(4)]
        tile_oh = [onehots[:, 4 * P + j * NT:4 * P + (j + 1) * NT] for j in range(4)]
        zero = gate_parts[:, 0:P]
        node_id = gate_parts[:, P:P + NB]

        psA = [psum("psA0"), psum("psA1")]
        psH = [psum("psH0"), psum("psH1")]
        psE = [psum("psE0"), psum("psE1")]
        psG = psum("psG")
        psR = psum("psR")
        psQ = [psR, psG]

        s_ln_load = [sem(f"ln_load{c}") for c in range(LN_CHUNKS)]
        s_ln_stat = sem("ln_stat")
        s_ln_coef = sem("ln_coef")
        s_ln_applied = sem("ln_applied")
        s_xn_stored = sem("xn_stored")
        s_edges = sem("edges_loaded")
        s_consts = sem("consts_loaded")
        s_small = sem("small_loaded")
        s_pool_c = sem("pool_consts")
        s_tab = sem("tables_dve")
        s_masks = sem("step_masks_ready")
        s_tabs = sem("tables_ready")
        s_onehot = sem("expert_onehot_ready")
        s_pos = sem("positions_ready")
        s_cnt_mm = sem("count_matmul")
        s_staged = sem("staged")
        s_pass = sem("pool_waits_passed")
        s_pass_dve = sem("dve_waits_passed")
        s_gath = [sem(f"gathered{h}") for h in range(SECTIONS)]
        s_sel = sem("sel_ready")
        s_edge_mm = sem("edge_matmul_done")
        s_narrow_eq = sem("narrow_onehots")
        s_narrow = sem("narrow_sels_ready")
        s_parts = sem("quad_parts_ready")
        s_placed = sem("quad_placed")
        s_acc = sem("accumulated")

        s_aggs = sem("aggs_ready")
        s_ffn = sem("ffn_dve")
        s_z = sem("z_done")
        s_xg = sem("xg_loaded")
        s_x2_st = sem("x2_stored")
        s_lg = sem("logits_ready")
        s_xn2 = sem("xn2_ready")
        s_xt = sem("xn2T_transposed")
        s_xtc = sem("xn2T_copied")
        s_h = sem("hidden_matmul_done")
        s_gelu = sem("gelu_done")
        s_tr = sem("hidden_transposed")
        s_ev = sem("hidden_row_copied")
        s_gp = sem("gate_parts_done")
        s_gc = sem("gate_parts_copied")
        s_g = sem("gate_done")
        s_rows = sem("rows_ready")
        s_rows_free = sem("rows_free")
        s_rows_st = sem("rows_stored")

        s_main = sem("main_done")
        s_wd = sem("wd_loaded")
        s_bd = sem("bd_loaded")
        s_rt = sem("route_dve")
        s_rank = sem("rank_matmul")
        s_oh = sem("perm_onehots")
        s_pm = sem("perm_matmul")
        s_perm = sem("perm_ready")

        s_r2free = sem("routed_row_free")
        s_st2 = sem("routed_staged")
        s_g2 = [sem(f"routed_gathered{i}") for i in range(RING2)]
        s_t2 = sem("routed_transposed")
        s_c2 = sem("routed_copied")
        s_y2 = sem("routed_product")
        s_o2 = sem("routed_out_ready")
        s_n2 = sem("routed_negmax")
        s_e2 = sem("routed_expsum")
        s_d2 = sem("routed_prob")
        s_tl = sem("routed_product_read")
        s_st = [sem(f"routed_stored{i}") for i in range(RING2)]

        grow = [rows[:, i, :] for i in range(RING2)]
        hT2 = [hidT[:, i * 2:i * 2 + 2, :].rearrange("p a b -> p (a b)").rearrange("p (c s) -> p c s", c=HC)
               for i in range(RING2)]
        ybuf = [xg[:, i, :] for i in range(RING2)]
        tbuf = [xn2[:, i, :] for i in range(RING2)]
        st_in = stage[:, 0, 0:RING2]
        st_out = sb("st_out", [P, RING2], I32)
        negmax = sb("negmax", [P, RING2])
        expv = sb("expv", [P, RING2, E])
        esum = sb("esum", [P, RING2])
        prob = sb("prob", [P, RING2])
        psT2 = [psA, psH, psE, [psG, psR]]
        psY2 = [psT2[i][0][:, 0:C] for i in range(RING2)]

        def load_values(ap, engine, top):
            return nc.values_load_multi_w_load_instructions(ap, engines=(engine,), min_val=0, max_val=top)[1]

        def load_columns(ap, engine, top):
            return nc.values_load_multi_w_load_instructions(
                ap, engines=(engine,), min_val=0, max_val=top,
                skip_runtime_bounds_check_because="columns are worked out modulo the ring's size")[1]

        block = ctx.enter_context(nc.Block())

        @block.sync
        def _(sp):
            xr = x.rearrange("(p r) c -> p r c", p=P)
            for c in range(LN_CHUNKS):
                sp.dma_start(ln_rows[:, c * LN_ROWS:(c + 1) * LN_ROWS, :],
                             xr[:, c * LN_ROWS:(c + 1) * LN_ROWS, :]).then_inc(s_ln_load[c], 16)
                if c == 0:
                    sp.dma_start(dst_i, dstT[:, :]).then_inc(s_edges, 16)
                    sp.dma_start(base_i, dstT[0, :].partition_broadcast(P)).then_inc(s_edges, 16)
            sp.dma_start(w_f[:, :], wT[:, :]).then_inc(s_consts, 16)
            sp.dma_start(src_i[:, :], srcT[:, :]).then_inc(s_consts, 16)
            sp.dma_start(wt[:, :, :], gnn_WT.rearrange("(k p) o -> p k o", p=P)).then_inc(s_consts, 16)
            sp.dma_start(w1[:, :, :], W1.rearrange("(k p) h -> p k h", p=P)).then_inc(s_consts, 16)
            sp.dma_start(wg[:, :, :], Wg.rearrange("(c p) e -> p c e", p=P)).then_inc(s_consts, 16)
            sp.dma_start(b1[:, :], b1T[:, :]).then_inc(s_consts, 16)
            sp.dma_start(gnn_b_bc[:, :], gnn_b.partition_broadcast(P)).then_inc(s_consts, 16)
            sp.dma_start(bg_bc[:, :], bg.partition_broadcast(P)).then_inc(s_consts, 16)
            sp.wait_ge(s_consts, 16 * 8)
            sp.sem_inc(s_small, 1)
            sp.sem_inc(s_rows_free, 1)
            sp.wait_ge(s_xn_stored, 16 * LN_CHUNKS)
            sp.dma_start(xg[:, :, :], x[0:GROUP, :].rearrange("(q p) c -> p q c", p=P)).then_inc(s_xg, 16)

            def store_x2(f):
                sp.wait_ge(s_xn2, f + 1)
                sp.dma_start(row_dram[bass.ds(f * GROUP, GROUP), 0:C].rearrange("(q p) c -> p q c", p=P),
                             xg[:, :, :]).then_inc(s_x2_st, 16)
                sp.wait_ge(s_x2_st, f * 16 + 16)

            def load_x(f):
                sp.dma_start(xg[:, :, :], x[bass.ds(f * GROUP, GROUP), :]
                             .rearrange("(q p) c -> p q c", p=P)).then_inc(s_xg, 16)

            def store_rows(f):
                sp.wait_ge(s_rows, f + 1)
                sp.dma_start(row_dram[bass.ds(f * GROUP, GROUP), C:ROW].rearrange("(q p) c -> p q c", p=P),
                             rows[:, :, C:ROW]).then_inc(s_rows_st, 16)
                sp.wait_ge(s_rows_st, f * 16 + 16)
                sp.sem_inc(s_rows_free, 1)

            store_x2(0)
            load_x(1)
            with sp.Fori(0, NF - 2) as f:
                store_x2(f + 1)
                load_x(f + 2)
                store_rows(f)
            store_x2(NF - 1)
            store_rows(NF - 2)
            store_rows(NF - 1)
            sp.wait_ge(s_main, 1)
            for e in range(E):
                sp.dma_start(wd[:, e * HC:(e + 1) * HC, :],
                             Wd[e].rearrange("(c p) o -> p c o", p=P)).then_inc(s_wd, 16)
            sp.dma_start(bd_bc, bd.rearrange("e c -> (e c)").partition_broadcast(P)).then_inc(s_bd, 16)

        @block.gpsimd
        def _(pool):
            nc.gpsimd.memset(ones[:, :], 1.0).then_inc(s_pool_c, 1)
            nc.gpsimd.iota(iota_i[:, :], [[1, IOTA]], base=0, channel_multiplier=0).then_inc(s_pool_c, 1)
            nc.gpsimd.iota(part_i[:, :], [[0, 1]], base=0, channel_multiplier=1).then_inc(s_pool_c, 1)
            pool.wait_ge(s_pool_c, 3)
            nc.gpsimd.affine_select(out=ident[:, :], in_=ones[:, :], compare_op=ALU.is_equal, fill=0.0,
                                    base=0, pattern=[[-1, P]], channel_multiplier=1).then_inc(s_pool_c, 1)
            nc.gpsimd.affine_select(out=upper[:, :], in_=ones[:, :], compare_op=ALU.is_gt, fill=0.0,
                                    base=0, pattern=[[1, P]], channel_multiplier=-1).then_inc(s_pool_c, 1)
            pool.wait_ge(s_small, 1)
            pool.wait_ge(s_xn_stored, 16 * LN_CHUNKS)
            with pool.Fori(0, NG // SECTIONS) as i:
                for h in range(SECTIONS):
                    pool.wait_ge(s_edge_mm, i * (SECTIONS * STEP_TILES) + (h + 1) * STEP_TILES)
                    pool.sem_inc(s_pass, 1)
                    nc.gpsimd.tensor_copy(stage[:, h, :],
                                          src_i[:, bass.ds(i * (SECTIONS * STEP_TILES) + h * STEP_TILES, STEP_TILES)]
                                          ).then_inc(s_staged, 1)
                    pool.wait_ge(s_staged, i * SECTIONS + h + 1)
                    pool.sem_inc(s_pass, 1)
                    for j in range(STEP_TILES):
                        nc.gpsimd.indirect_dma_start(
                            out=xring[:, h * STEP_TILES + j, :], out_offset=None, in_=xn_dram[:, :],
                            in_offset=bass.IndirectOffsetOnAxis(ap=stage[:, h, j:j + 1], axis=0)
                        ).then_inc(s_gath[h], 16)

            def gather_routed(t, i):
                pool.wait_ge(s_r2free, t + 1)
                pool.sem_inc(s_pass, 1)
                nc.gpsimd.tensor_copy(st_in[:, i:i + 1], perm_i[:, bass.ds(t, 1)]).then_inc(s_st2, 1)
                pool.wait_ge(s_st2, t + 1)
                pool.sem_inc(s_pass, 1)
                nc.gpsimd.indirect_dma_start(
                    out=grow[i], out_offset=None, in_=row_dram[:, :],
                    in_offset=bass.IndirectOffsetOnAxis(ap=st_in[:, i:i + 1], axis=0)).then_inc(s_g2[i], 16)

            def scatter_routed(t, i):
                pool.wait_ge(s_o2, t + 1)
                pool.sem_inc(s_pass, 1)
                nc.gpsimd.indirect_dma_start(
                    out=out[:, :], out_offset=bass.IndirectOffsetOnAxis(ap=st_out[:, i:i + 1], axis=0),
                    in_=ybuf[i], in_offset=None, bounds_check=N - 1, oob_is_err=False).then_inc(s_st[i], 16)

            pool.wait_ge(s_perm, 1)
            pool.wait_ge(s_rows_free, NF + 1)
            for i in range(RING2):
                gather_routed(i, i)
            with pool.Fori(0, ROUNDS - 1) as r:
                for i in range(RING2):
                    gather_routed(r * RING2 + RING2 + i, i)
                    scatter_routed(r * RING2 + i, i)
            for t in range((ROUNDS - 1) * RING2, NT):
                if t + RING2 < NT:
                    gather_routed(t + RING2, t % RING2)
                scatter_routed(t, t % RING2)
            for i in range(RING2):
                pool.wait_ge(s_st[i], 16 * (-(-(NT - i) // RING2)))

        @block.scalar
        def _(act):
            xnr = xn_dram.rearrange("(p r) c -> p r c", p=P)
            for c in range(LN_CHUNKS):
                act.wait_ge(s_ln_coef, c + 1)
                with act.Fori(0, 2) as r2:
                    for j in range(LN_ROWS // 2):
                        r = bass.ds(r2 * (LN_ROWS // 2) + c * LN_ROWS + j, 1)
                        nc.scalar.activation(ln_rows[:, r, :], ln_rows[:, r, :], ACT.Identity, bias=nmr[:, r],
                                             scale=rstd[:, r]).then_inc(s_ln_applied, 1)
                act.wait_ge(s_ln_applied, (c + 1) * LN_ROWS)
                act.dma_start(xnr[:, c * LN_ROWS:(c + 1) * LN_ROWS, :],
                              ln_rows[:, c * LN_ROWS:(c + 1) * LN_ROWS, :]).then_inc(s_xn_stored, 16)
            act.wait_ge(s_small, 1)
            def copy_xn2T(f):
                for k in range(KC):
                    act.wait_ge(s_xt, f * KC + k + 1)
                    nc.scalar.activation(xn2T[:, k, :], psH[k][:, :], ACT.Identity).then_inc(s_xtc, 1)

            def hidden(f):
                for c in range(HC):
                    act.wait_ge(s_h, f * HC + c + 1)
                    nc.scalar.activation(hidT[:, c, :], psH[c % 2][:, :], ACT.Gelu,
                                         bias=b1[:, c:c + 1]).then_inc(s_gelu, 1)
                act.wait_ge(s_gp, f + 1)
                nc.scalar.activation(gate_parts[:, :], psG[:, :], ACT.Identity).then_inc(s_gc, 1)

            copy_xn2T(0)
            with act.Fori(0, NF - 1) as f:
                hidden(f)
                copy_xn2T(f + 1)
            hidden(NF - 1)

            def routed_act(t, i):
                for k in range(2):
                    act.wait_ge(s_t2, t * 2 + k + 1)
                    nc.scalar.activation(hT2[i][:, k * 4:k * 4 + 4, :],
                                         psT2[i][k][:, :].rearrange("p (c s) -> p c s", c=4),
                                         ACT.Identity).then_inc(s_c2, 1)
                act.wait_ge(s_n2, t + 1)
                nc.scalar.activation(expv[:, i, :], grow[i][:, LOGITS:ROW], ACT.Exp,
                                     bias=negmax[:, i:i + 1], accum_out=esum[:, i:i + 1]).then_inc(s_e2, 1)

            with act.Fori(0, ROUNDS) as r:
                for i in range(RING2):
                    routed_act(r * RING2 + i, i)
            for t in range(ROUNDS * RING2, NT):
                routed_act(t, t % RING2)

        @block.tensor
        def _(pe):
            pe.sem_inc(s_edge_mm, MM0)
            pe.wait_ge(s_pool_c, 5)
            pe.wait_ge(s_masks, 1)
            nc.tensor.matmul(psG[:, 0:2 * STEPS + 2 * NG], ones[:, :], step_masks,
                             start=True, stop=True).then_inc(s_cnt_mm, 1)
            pe.wait_ge(s_small, 1)
            pe.wait_ge(s_tabs, 1)
            def gather_step(g, h):
                pe.wait_ge(s_gath[h], (g + (SECTIONS - h)) * STEP_TILES * 16 // SECTIONS)
                wide, = load_columns(quads_i[0:1, bass.ds(g, 1), 0:1].rearrange("a b c -> a (b c)"), PE, 1)
                with pe.If(wide == 0):
                    def partial(q):
                        pe.wait_ge(s_narrow, g * 2 + q // 2 + 1)
                        for j in range(QUAD):
                            t = h * STEP_TILES + q * QUAD + j
                            mm = nc.tensor.matmul(psQ[q % 2][j * LANES:(j + 1) * LANES, 0:C], sel_narrow[:, t, :],
                                                  xring[:, t, :], start=True, stop=True)
                        mm.then_inc(s_edge_mm, QUAD)

                    def place_quad(q):
                        pe.wait_ge(s_parts, g * QUADS + q + 1)
                        for k in range(KC):
                            mm = nc.tensor.matmul(psE[q % 2][:, k * NARROW:(k + 1) * NARROW],
                                                  parts[:, q % 2, k * P:(k + 1) * P], place[:, q, :],
                                                  start=True, stop=True)
                        mm.then_inc(s_placed, 1)

                    partial(0)
                    for q in range(1, QUADS):
                        partial(q)
                        place_quad(q - 1)
                    place_quad(QUADS - 1)
                with pe.If(wide == 1):
                    for j in range(STEP_TILES):
                        n = g * STEP_TILES + j
                        pe.wait_ge(s_sel, n + 1)
                        pe.wait_ge(s_acc, n + ACC0 - 1)
                        for k in range(KC):
                            mm = nc.tensor.matmul(psE[j % 2][:, k * P:(k + 1) * P],
                                                  xring[:, h * STEP_TILES + j, k * P:(k + 1) * P],
                                                  sel[:, j % S_RING, :], start=True, stop=True)
                        mm.then_inc(s_edge_mm, 1)
                    pe.sem_inc(s_placed, QUADS)

            def messages(f):
                pe.wait_ge(s_aggs, f + 1)
                for q in range(QB):
                    for k in range(KC):
                        mm = nc.tensor.matmul(psA[q // 2][:, (q % 2) * C:(q % 2 + 1) * C],
                                              aggs[:, k, q * P:(q + 1) * P], wt[:, k, :],
                                              start=(k == 0), stop=(k == KC - 1))
                mm.then_inc(s_z, 1)

            def transpose_xn2(f):
                pe.wait_ge(s_xn2, f + 1)
                for k in range(KC):
                    for q in range(QB):
                        mm = nc.tensor.transpose(psH[k][:, q * P:(q + 1) * P],
                                                 xn2[:, q, k * P:(k + 1) * P], ident[:, :])
                    mm.then_inc(s_xt, 1)

            def hidden(f, in_loop):
                pe.wait_ge(s_xtc, f * KC + KC)
                for c in range(HC):
                    if c >= 2:
                        pe.wait_ge(s_gelu, f * HC + c - 1)
                    for k in range(KC):
                        mm = nc.tensor.matmul(psH[c % 2][:, :], w1[:, k, c * P:(c + 1) * P], xn2T[:, k, :],
                                              start=(k == 0), stop=(k == KC - 1))
                    mm.then_inc(s_h, 1)
                pe.wait_ge(s_gelu, f * HC + HC)
                for c in range(HC):
                    cg = c % 4
                    mm = nc.tensor.matmul(psG[cg * GATE_COLS:(cg + 1) * GATE_COLS, :], wg[:, c, :], hidT[:, c, :],
                                          start=(c < 4), stop=(c >= 4))
                mm.then_inc(s_gp, 1)
                if in_loop:
                    pe.wait_ge(s_xn2, f + 2)
                else:
                    pe.wait_ge(s_ev, f * (2 * QB))
                for i in range(2 * QB):
                    half, q = i // QB, i % QB
                    if i >= 2:
                        pe.wait_ge(s_ev, f * (2 * QB) + i - 1)
                    for j in range(4):
                        mm = nc.tensor.transpose(psA[i % 2][:, j * P:(j + 1) * P],
                                                 hidT[:, 4 * half + j, q * P:(q + 1) * P], ident[:, :])
                    mm.then_inc(s_tr, 1)
                pe.wait_ge(s_gc, f + 1)
                for q in range(QB):
                    mm = nc.tensor.matmul(psE[0][:, q * E:(q + 1) * E], gate_parts[:, q * P:(q + 1) * P],
                                          fold[:, :], start=True, stop=True)
                mm.then_inc(s_g, 1)

            with pe.Fori(0, STEPS) as k:
                kind, g, f = load_values(steps_i[0:1, bass.ds(k, 1), 0:3].rearrange("a b c -> a (b c)"), PE, NG)
                g, f = g.with_bounds(min_val=0, max_val=NG - 1), f.with_bounds(min_val=0, max_val=NF - 1)
                for h in range(SECTIONS):
                    with pe.If(kind == h):
                        gather_step(g, h)
                with pe.If(kind == SECTIONS):
                    messages(f)
                    with pe.If(f > 0):
                        before, = load_values(steps_i[0:1, bass.ds(k, 1), 5:6].rearrange("a b c -> a (b c)"), PE,
                                              NF - 1)
                        hidden(before, True)
                    transpose_xn2(f)
            hidden(NF - 1, False)

            pe.wait_ge(s_onehot, 1)
            oh = scr[:, 0:E * NB]
            for h in range(2):
                nc.tensor.matmul(psA[h][:, 0:4 * NB], upper[:, :], oh[:, h * 4 * NB:(h + 1) * 4 * NB],
                                 start=True, stop=True)
                mm = nc.tensor.matmul(psH[h][:, 0:4 * NB], ones[:, :], oh[:, h * 4 * NB:(h + 1) * 4 * NB],
                                      start=True, stop=True)
            mm.then_inc(s_rank, 1)
            pe.wait_ge(s_pos, 1)
            nc.tensor.matmul(psG[:, 0:NT], zero, tile_oh[0], start=True, stop=False).then_inc(s_pm, 4)
            with pe.Fori(0, NB // 4) as b4:
                for j in range(4):
                    pe.wait_ge(s_oh, b4 * 4 + j + 1)
                    nc.tensor.matmul(psG[:, 0:NT], slot_oh[j], tile_oh[j], start=False,
                                     stop=False).then_inc(s_pm, 1)
            nc.tensor.matmul(psG[:, 0:NT], zero, tile_oh[0], start=False, stop=True).then_inc(s_pm, 1)

            def transposes(t3, i):
                pe.wait_ge(s_g2[i], t3 * 16 + 16)
                for k in range(2):
                    for j in range(4):
                        c = 4 * k + j
                        mm = nc.tensor.transpose(psT2[i][k][:, j * P:(j + 1) * P],
                                                 grow[i][:, C + c * P:C + (c + 1) * P], ident[:, :])
                    mm.then_inc(s_t2, 1)

            def product(t, i):
                e8 = pe.value_load(texp_i[0:1, bass.ds(t, 1), 0:1].rearrange("a b c -> a (b c)"),
                                   min_val=0, max_val=(E - 1) * HC)
                pe.wait_ge(s_c2, t * 2 + 2)
                for c in range(HC):
                    mm = nc.tensor.matmul(psY2[i], hT2[i][:, c, :], wd[:, bass.ds(e8 + c, 1), :],
                                          start=(c == 0), stop=(c == HC - 1))
                mm.then_inc(s_y2, 1)

            pe.wait_ge(s_perm, 1)
            pe.wait_ge(s_wd, 16 * E)
            transposes(0, 0)
            with pe.Fori(0, ROUNDS - 1) as r:
                for i in range(RING2):
                    transposes(r + (i + 1) // RING2, (i + 1) % RING2)
                    product(r * RING2 + i, i)
            for t in range((ROUNDS - 1) * RING2, NT):
                if t + 1 < NT:
                    transposes((t + 1) // RING2, (t + 1) % RING2)
                product(t, t % RING2)

        @block.vector
        def _(dve):
            def moments(link, mv):
                n = mv.shape[1]
                diff, squares = nhalf[:, 0:n], newton[:, 0:n]
                nc.vector.tensor_tensor(mv[:, :, 0], stats[:, 0:n, 1], stats[:, 0:n, 4], ALU.add)
                nc.vector.tensor_tensor(squares, stats[:, 0:n, 2], stats[:, 0:n, 5], ALU.add)
                link(nc.vector.tensor_tensor(diff, stats[:, 0:n, 1], stats[:, 0:n, 4], ALU.subtract))
                nc.vector.tensor_scalar(mv[:, :, 0], mv[:, :, 0], 0.5, None, ALU.mult)
                link(nc.vector.scalar_tensor_tensor(out=diff, in0=diff, scalar=0.25, in1=diff,
                                                    op0=ALU.mult, op1=ALU.mult))
                link(nc.vector.scalar_tensor_tensor(out=mv[:, :, 1], in0=squares, scalar=1.0 / C, in1=diff,
                                                    op0=ALU.mult, op1=ALU.add))

            def rsqrt(link, y, var):
                n = y.shape[1]
                v, a = nhalf[:, 0:n], newton[:, 0:n]
                link(nc.vector.tensor_scalar(v, var, EPS, None, ALU.add))
                link(nc.vector.tensor_scalar(a.bitcast(I32), v.bitcast(I32), 1, None, ALU.logical_shift_right))
                link(nc.vector.tensor_scalar(y.bitcast(I32), a.bitcast(I32), -1.0, RSQRT_MAGIC, ALU.mult, ALU.add))
                link(nc.vector.tensor_scalar(v, v, -0.5, None, ALU.mult))
                for _ in range(3):
                    link(nc.vector.tensor_tensor(a, y, y, ALU.mult))
                    link(nc.vector.tensor_tensor(a, a, v, ALU.mult))
                    link(nc.vector.scalar_tensor_tensor(out=y, in0=a, scalar=1.5, in1=y, op0=ALU.add, op1=ALU.mult))

            tick = Ticker(dve, s_tab, 0)
            for c in range(LN_CHUNKS):
                dve.wait_ge(s_ln_load[c], 16)
                for j in range(LN_ROWS):
                    nc.vector.bn_stats(stats[:, j, :], ln_rows[:, c * LN_ROWS + j, :]).then_inc(s_ln_stat, 1)
                dve.wait_ge(s_ln_stat, (c + 1) * LN_ROWS)
                moments(tick, meanvar[:, c * LN_ROWS:(c + 1) * LN_ROWS, :])
                cs = slice(c * LN_ROWS, (c + 1) * LN_ROWS)
                rsqrt(tick, rstd[:, cs], meanvar[:, cs, 1])
                nc.vector.scalar_tensor_tensor(out=nmr[:, cs], in0=meanvar[:, cs, 0], scalar=-1.0,
                                               in1=rstd[:, cs], op0=ALU.mult, op1=ALU.mult).then_inc(s_ln_coef, 1)
            dve.wait_ge(s_pool_c, 5)
            dve.wait_ge(s_edges, 32)
            nc.vector.memset(zero_col[:, :], 0.0)
            nc.vector.tensor_copy(iota[:, :], iota_i[:, :])
            nc.vector.tensor_copy(part[:, :], part_i[:, :])
            lane_i = newton[:, 0:1].bitcast(I32)
            tick(nc.vector.tensor_scalar(lane_i, part_i[:, :], GATE_COLS - 1, None, ALU.bitwise_and))
            tick(nc.vector.tensor_copy(nhalf[:, 0:1], lane_i))
            nc.vector.tensor_scalar(fold[:, :], iota[:, 0:E], nhalf[:, 0:1], None, ALU.is_equal)
            base_q = base_i[:, 0:TILES].rearrange("p (q j) -> p q j", j=QUAD)
            for j in range(QUAD):
                rows_j = slice(j * LANES, (j + 1) * LANES)
                o = nc.vector.tensor_tensor(shift_f[rows_j, :], base_q[rows_j, :, j], base_q[rows_j, :, 0],
                                            ALU.subtract)
            tick(o)
            nc.vector.tensor_scalar(shift_f[:, :], shift_f[:, :], nhalf[:, 0:1], None, ALU.add)
            tick(nc.vector.tensor_tensor(rel_f[:, :], dst_i, base_i, ALU.subtract))
            last_lane = newton[:, 1:2]
            nc.vector.tensor_scalar(last_lane, part[:, :], float(P - 1), None, ALU.is_equal)
            nc.vector.tensor_reduce(span_tile, rel_f[:, 0:TILES].rearrange("p (g t) -> p g t", t=STEP_TILES), AX.X,
                                    ALU.max)
            tick(nc.vector.tensor_tensor(slot_f[:, 0:TILES // QUAD],
                                         dst_i[:, 0:TILES].rearrange("p (q j) -> p q j", j=QUAD)[:, :, QUAD - 1],
                                         base_q[:, :, 0], ALU.subtract))
            tick(nc.vector.tensor_reduce(span_quad, slot_f[:, 0:TILES // QUAD].rearrange("p (g q) -> p g q", q=QUADS),
                                         AX.X, ALU.max))
            for a, span in enumerate((span_tile, span_quad)):
                nc.vector.tensor_scalar(step_masks[:, 2 * STEPS + a * NG:2 * STEPS + (a + 1) * NG], span,
                                        last_lane, None, ALU.mult)
            tick(nc.vector.tensor_copy(base_f, base_i[:, 0:TILES]))
            tick(nc.vector.tensor_scalar(stats[:, 0, 0:1], part[:, :], float(GROUP), float(GROUP),
                                         ALU.mult, ALU.add))
            tick(nc.vector.tensor_scalar(slot_f, base_f, stats[:, 0, 0:1], 0.0, ALU.is_lt, ALU.add,
                                         accum_out=stats[:, 1, 0:1]))
            steps_of = stats[:, 2, 0:1].bitcast(I32)
            tick(nc.vector.tensor_scalar(steps_of, stats[:, 1, 0:1], float(STEP_TILES - 1), None, ALU.add))
            tick(nc.vector.tensor_scalar(steps_of, steps_of, STEP_TILES.bit_length() - 1, None,
                                         ALU.logical_shift_right))
            tick(nc.vector.tensor_tensor(stats[:, 4, 0:1], steps_of, part[:, :], ALU.add))
            nc.vector.tensor_scalar(step_masks[:, 0:STEPS], iota[:, 0:STEPS], stats[:, 4, 0:1], None, ALU.is_equal)
            nc.vector.tensor_scalar(step_masks[:, STEPS:2 * STEPS], iota[:, 0:STEPS], stats[:, 4, 0:1], None,
                                    ALU.is_gt).then_inc(s_masks, 1)
            log_group = GROUP.bit_length() - 1
            nc.vector.tensor_scalar(rem_i, base_i[0:1, 0:TILES], GROUP - 1, None, ALU.bitwise_and)
            tick(nc.vector.tensor_scalar(slot_i, base_i[0:1, 0:TILES], log_group, NS - 1, ALU.logical_shift_right,
                                         ALU.bitwise_and))
            tick(nc.vector.scalar_tensor_tensor(out=off_i[0:1, :], in0=slot_i, scalar=float(SLOT),
                                                in1=rem_i, op0=ALU.mult, op1=ALU.add))
            spans = [psG[0:1, 2 * STEPS + a * NG:2 * STEPS + (a + 1) * NG] for a in range(2)]
            dve.wait_ge(s_cnt_mm, 1)
            nc.vector.tensor_scalar(span_tile[0:1, :], spans[0], float(LANES), None, ALU.is_ge)
            tick(nc.vector.tensor_scalar(span_quad[0:1, :], spans[1], float(NARROW), None, ALU.is_ge))
            nc.vector.tensor_tensor(quads_i[0:1, :, 0], span_tile[0:1, :], span_quad[0:1, :], ALU.max)
            nc.vector.tensor_copy(quads_i[0:1, :, 1:1 + QUADS],
                                  off_i[0:1, :].rearrange("p (g q j) -> p g q j", q=QUADS, j=QUAD)[:, :, :, 0])
            next_i, third = quads_i[0:1, :, 1 + QUADS], span_tile[0:1, :].bitcast(I32)
            tick(nc.vector.tensor_scalar(next_i, iota_i[0:1, 0:NG], 1.0, None, ALU.add))
            tick(nc.vector.tensor_scalar(third, next_i, 171.0, None, ALU.mult))
            tick(nc.vector.tensor_scalar(third, third, 9, None, ALU.logical_shift_right))
            tick(nc.vector.scalar_tensor_tensor(out=next_i, in0=third, scalar=-float(SECTIONS), in1=next_i,
                                                op0=ALU.mult, op1=ALU.add))
            nc.vector.tensor_scalar(next_i, next_i, float(STEP_TILES * LANES), None, ALU.mult)
            nc.vector.tensor_copy(u[2].bitcast(I32), psG[:, 0:STEPS])
            tick(nc.vector.tensor_copy(u[3].bitcast(I32), psG[:, STEPS:2 * STEPS]))
            is_group, groups, gathers, section, prev = (a.bitcast(I32) for a in (u[2], u[3], u[4], u[5], u[0]))
            nc.vector.tensor_scalar(prev, groups, float(NS - 1), None, ALU.add)
            tick(nc.vector.tensor_tensor(gathers, iota_i[:, 0:STEPS], groups, ALU.subtract))
            nc.vector.tensor_scalar(prev, prev, NS - 1, None, ALU.bitwise_and)
            nc.vector.tensor_scalar(u[6].bitcast(I32), groups, NS - 1, None, ALU.bitwise_and)
            tick(nc.vector.tensor_scalar(section, gathers, 171.0, None, ALU.mult))
            tick(nc.vector.tensor_scalar(section, section, 9, None, ALU.logical_shift_right))
            tick(nc.vector.scalar_tensor_tensor(out=section, in0=section, scalar=-float(SECTIONS), in1=gathers,
                                                op0=ALU.mult, op1=ALU.add))
            nc.vector.scalar_tensor_tensor(out=steps_i[:, :, 0], in0=is_group, scalar=float(SECTIONS), in1=section,
                                           op0=ALU.mult, op1=ALU.max)
            nc.vector.tensor_copy(steps_i[:, :, 1], gathers)
            nc.vector.tensor_copy(steps_i[:, :, 2], groups)
            nc.vector.tensor_scalar(steps_i[:, :, 5], groups, -1.0, 0.0, ALU.add, ALU.max)
            nc.vector.tensor_scalar(steps_i[:, :, 3], u[6].bitcast(I32), float(SLOT), None, ALU.mult)
            tick(nc.vector.tensor_scalar(steps_i[:, :, 4], prev, float(SLOT), float(GROUP), ALU.mult, ALU.add))
            dve.wait_ge(s_small, 1)

            def narrow_onehots(g, start, half):
                n = STEP_TILES // 2
                nc.vector.tensor_tensor(
                    selv[:, bass.ds(start + half * n * LANES, n * LANES)].rearrange("p (t n) -> p t n", n=LANES),
                    iota[:, 0:LANES].unsqueeze(1).to_broadcast([P, n, LANES]),
                    rel_f[:, bass.ds(g * STEP_TILES + half * n, n)].unsqueeze(2).to_broadcast([P, n, LANES]),
                    ALU.is_equal).then_inc(s_narrow_eq, 1)

            def narrow_weights(g, start, half):
                n = STEP_TILES // 2
                both = selv[:, bass.ds(start + half * n * LANES, n * LANES)].rearrange("p (t n) -> p t n", n=LANES)
                dve.wait_ge(s_narrow_eq, g * 2 + half + 1)
                nc.vector.tensor_tensor(
                    both, both,
                    w_f[:, bass.ds(g * STEP_TILES + half * n, n)].unsqueeze(2).to_broadcast([P, n, LANES]),
                    ALU.mult).then_inc(s_narrow, 1)

            for half in range(2):
                narrow_onehots(0, 0, half)
            for half in range(2):
                narrow_weights(0, 0, half)
            dve.wait_ge(s_xn_stored, 16 * LN_CHUNKS)
            nc.vector.memset(agg, 0.0).then_inc(s_acc, ACC0)
            dve.wait_ge(s_acc, ACC0)
            nc.vector.memset(stats[:, :, :], 0.0).then_inc(s_tabs, 1)

            def make_sel(g, j):
                col = g * STEP_TILES + j
                nc.vector.tensor_scalar(sel[:, j % S_RING, :], iota[:, 0:P], rel_f[:, bass.ds(col, 1)],
                                        w_f[:, bass.ds(col, 1)], ALU.is_equal, ALU.mult).then_inc(s_sel, 1)

            def gather_step(g):
                wide, *at, start = load_columns(quads_i[0:1, bass.ds(g, 1), :].rearrange("a b c -> a (b c)"), DVE,
                                        (NS - 1) * SLOT + GROUP - 1)
                start = start.with_bounds(min_val=0, max_val=(SECTIONS - 1) * STEP_TILES * LANES)
                with dve.If(wide == 0):
                    def copy_parts(q):
                        dve.wait_ge(s_edge_mm, g * STEP_TILES + (q + 1) * QUAD + MM0)
                        nc.vector.tensor_copy(parts[:, q % 2, :], psQ[q % 2][:, 0:C]).then_inc(s_parts, 1)

                    def accumulate(q):
                        dve.wait_ge(s_placed, g * QUADS + q + 1)
                        dve.wait_ge(s_acc, g * STEP_TILES + q * QUAD + ACC0)
                        win = agg[:, :, bass.ds(at[q], NARROW)]
                        nc.vector.tensor_tensor(win, psE[q % 2][:, 0:KC * NARROW].rearrange("p (k n) -> p k n", k=KC),
                                                win, ALU.add).then_inc(s_acc, QUAD)

                    nc.vector.tensor_tensor(
                        place[:, :, :], iota[:, 0:NARROW].unsqueeze(1).to_broadcast([P, QUADS, NARROW]),
                        shift_f[:, bass.ds(g * QUADS, QUADS)].unsqueeze(2).to_broadcast([P, QUADS, NARROW]),
                        ALU.is_equal)
                    copy_parts(0)
                    narrow_onehots(g + 1, start, 0)
                    copy_parts(1)
                    narrow_weights(g + 1, start, 0)
                    accumulate(0)
                    copy_parts(2)
                    narrow_onehots(g + 1, start, 1)
                    accumulate(1)
                    copy_parts(3)
                    narrow_weights(g + 1, start, 1)
                    accumulate(2)
                    accumulate(3)
                    dve.sem_inc(s_sel, STEP_TILES)
                with dve.If(wide == 1):
                    offs = load_columns(off_i[0:1, bass.ds(g * STEP_TILES, STEP_TILES)], DVE,
                                       (NS - 1) * SLOT + GROUP - 1)
                    for j in range(S_RING // 2):
                        make_sel(g, j)
                    for j in range(STEP_TILES):
                        if j + S_RING // 2 < STEP_TILES:
                            make_sel(g, j + S_RING // 2)
                        n = g * STEP_TILES + j
                        dve.wait_ge(s_edge_mm, n + 1 + MM0)
                        dve.wait_ge(s_acc, n + ACC0)
                        win = agg[:, :, bass.ds(offs[j], P)]
                        nc.vector.tensor_tensor(win, psE[j % 2][:, 0:KC * P].rearrange("p (k n) -> p k n", k=KC),
                                                win, ALU.add).then_inc(s_acc, 1)
                    dve.sem_inc(s_parts, QUADS)
                    for half in range(2):
                        narrow_onehots(g + 1, start, half)
                        narrow_weights(g + 1, start, half)

            def first_part(f, g, slot, spill):
                dve.wait_ge(s_acc, g * STEP_TILES + ACC0)
                dve.sem_inc(s_pass_dve, 1)
                link = Ticker(dve, s_ffn, f * FFN_LINKS)
                here, before = agg[:, :, bass.ds(slot, GROUP)], agg[:, :, bass.ds(spill, P)]
                link(nc.vector.tensor_copy(aggs[:, :, :], here))
                nc.vector.tensor_tensor(aggs[:, :, 0:P], aggs[:, :, 0:P], before, ALU.add).then_inc(s_aggs, 1)
                dve.wait_ge(s_aggs, f + 1)
                nc.vector.tensor_scalar(here, zero_col[:, :].unsqueeze(2).to_broadcast([P, KC, GROUP]), 0.0, None,
                                        ALU.add)
                link(nc.vector.tensor_scalar(before, zero_col[:, :].unsqueeze(2).to_broadcast([P, KC, P]), 0.0,
                                             None, ALU.add))
                dve.wait_ge(s_z, f + 1)
                dve.wait_ge(s_xg, f * 16 + 16)
                x2 = xg[:, :, :]
                for a in range(2):
                    o = nc.vector.tensor_tensor(x2[:, 2 * a:2 * a + 2, :],
                                                psA[a][:, :].rearrange("p (q c) -> p q c", c=C),
                                                x2[:, 2 * a:2 * a + 2, :], ALU.add)
                link(o)
                link(nc.vector.tensor_tensor(x2, x2, gnn_b_bc[:, :].unsqueeze(1).to_broadcast([P, QB, C]), ALU.add))
                for q in range(QB):
                    o = nc.vector.bn_stats(stats[:, q, :], x2[:, q, :])
                link(o)
                moments(link, meanvar[:, 0:QB, :])
                rsqrt(link, rstd[:, 0:QB], meanvar[:, 0:QB, 1])
                for q in range(QB):
                    o = nc.vector.tensor_scalar(xn2[:, q, :], x2[:, q, :], meanvar[:, q, 0:1],
                                                rstd[:, q:q + 1], ALU.subtract, ALU.mult)
                o.then_inc(s_xn2, 1)
                assert link.n == FFN_LINKS, link.n

            def second_part(f):
                dve.wait_ge(s_rows_free, f + 1)
                dve.sem_inc(s_pass_dve, 1)
                for i in range(2 * QB):
                    half, q = i // QB, i % QB
                    dve.wait_ge(s_tr, f * (2 * QB) + i + 1)
                    nc.vector.tensor_copy(rows[:, q, C + half * 512:C + (half + 1) * 512],
                                          psA[i % 2][:, :]).then_inc(s_ev, 1)
                dve.wait_ge(s_g, f + 1)
                lg = rows[:, :, LOGITS:ROW]
                nc.vector.tensor_tensor(lg, psE[0][:, 0:QB * E].rearrange("p (q e) -> p q e", e=E),
                                        bg_bc[:, :].unsqueeze(1).to_broadcast([P, QB, E]), ALU.add
                                        ).then_inc(s_lg, 1)
                dve.wait_ge(s_lg, f + 1)
                dve.wait_ge(s_ev, f * (2 * QB) + 2 * QB)
                dve.sem_inc(s_pass_dve, 1)
                nc.vector.tensor_copy(logits[:, bass.ds(f * QB, QB), :], lg).then_inc(s_rows, 1)

            with dve.Fori(0, STEPS) as k:
                kind, g = load_values(steps_i[0:1, bass.ds(k, 1), 0:2].rearrange("a b c -> a (b c)"), DVE, NG)
                with dve.If(kind == SECTIONS):
                    f, = load_values(steps_i[0:1, bass.ds(k, 1), 2:3].rearrange("a b c -> a (b c)"), DVE, NF)
                    slot, spill = load_columns(steps_i[0:1, bass.ds(k, 1), 3:5].rearrange("a b c -> a (b c)"),
                                               DVE, NS * SLOT)
                    f = f.with_bounds(min_val=0, max_val=NF - 1)
                    slot = slot.with_bounds(min_val=0, max_val=(NS - 1) * SLOT)
                    spill = spill.with_bounds(min_val=0, max_val=(NS - 1) * SLOT + GROUP)
                    first_part(f, g.with_bounds(min_val=0, max_val=NG), slot, spill)
                    with dve.If(f > 0):
                        before, = load_values(steps_i[0:1, bass.ds(k, 1), 5:6].rearrange("a b c -> a (b c)"), DVE,
                                              NF - 1)
                        second_part(before)
                with dve.If(kind < SECTIONS):
                    gather_step(g.with_bounds(min_val=0, max_val=NG - 1))
            second_part(NF - 1)
            dve.wait_ge(s_acc, TILES + ACC0)
            dve.wait_ge(s_rows, NF)
            dve.wait_ge(s_gelu, NF * HC)
            dve.sem_inc(s_main, 1)

            route = Ticker(dve, s_rt, 0)
            nc.vector.memset(onehots, 0.0)
            nc.vector.memset(zero, 0.0)
            nc.vector.tensor_scalar(e_rank, iota[:, 0:E], -1.0, float(E), ALU.mult, ALU.add)
            nc.vector.tensor_scalar(tmp_b, iota[:, 0:NB], float(P), part[:, 0:1], ALU.mult, ALU.add)
            nc.vector.tensor_scalar(part1, part[:, :], float(PAD_ROW + 1), None, ALU.add)
            route(nc.vector.tensor_reduce(best, logits[:, :, :], AX.X, ALU.max))
            nc.vector.tensor_scalar(valid, tmp_b, float(N), None, ALU.is_lt)
            nc.vector.tensor_scalar(node_id, tmp_b, 1.0, None, ALU.add)
            route(nc.vector.tensor_tensor(score, logits[:, :, :], best.unsqueeze(2).to_broadcast([P, NB, E]),
                                          ALU.is_equal))
            route(nc.vector.tensor_tensor(score, score, e_rank.unsqueeze(1).to_broadcast([P, NB, E]), ALU.mult))
            route(nc.vector.tensor_reduce(best, score, AX.X, ALU.max))
            route(nc.vector.tensor_copy(total, e_rank.unsqueeze(2).to_broadcast([P, E, NB])))
            route(nc.vector.tensor_tensor(onehot, total, best.unsqueeze(1).to_broadcast([P, E, NB]), ALU.is_equal))
            nc.vector.tensor_tensor(onehot, onehot, valid.unsqueeze(1).to_broadcast([P, E, NB]),
                                    ALU.mult).then_inc(s_onehot, 1)
            dve.wait_ge(s_rank, 1)
            for h in range(2):
                o = nc.vector.tensor_copy(scr[:, 3 * E * NB + h * 4 * NB:3 * E * NB + (h + 1) * 4 * NB],
                                          psH[h][:, 0:4 * NB])
            route(o)
            for e in range(E):
                o = nc.vector.tensor_tensor_scan(incl[:, e, :], ones[:, 0:NB], total[:, e, :], 0.0,
                                                 ALU.mult, ALU.add)
            route(o)
            e_int = e_mod.bitcast(I32)
            route(nc.vector.tensor_scalar(e_int, incl[:, :, NB - 1], float(P - 1), None, ALU.add))
            route(nc.vector.tensor_scalar(e_int, e_int, ~(P - 1) & 0xFFFF, None, ALU.bitwise_and))
            route(nc.vector.tensor_copy(e_pad, e_int))
            route(nc.vector.tensor_tensor_scan(e_cum, ones[:, 0:E], e_pad, 0.0, ALU.mult, ALU.add))
            nc.vector.tensor_tensor(e_start, e_cum, e_pad, ALU.subtract)
            route(nc.vector.tensor_tensor(where, incl, total, ALU.subtract))
            for h in range(2):
                part_h = scr[:, 4 * E * NB + h * 4 * NB:4 * E * NB + (h + 1) * 4 * NB]
                o = nc.vector.tensor_tensor(part_h, psA[h][:, 0:4 * NB], part_h, ALU.add)
            route(o)
            route(nc.vector.tensor_tensor(where, where, e_start.unsqueeze(2).to_broadcast([P, E, NB]), ALU.add))
            route(nc.vector.tensor_tensor(where, where, onehot, ALU.mult))
            nc.vector.tensor_scalar(tmp_b, valid, -float(2 * NT * P), float(2 * NT * P), ALU.mult, ALU.add)
            route(nc.vector.tensor_reduce(pos, where.rearrange("p e b -> p b e"), AX.X, ALU.add))
            pos_i, slot_ib, tile_ib = (a.bitcast(I32) for a in (best, valid, tmp_b))
            route(nc.vector.tensor_tensor(pos_i, pos, tmp_b, ALU.add))
            nc.vector.tensor_scalar(slot_ib, pos_i, P - 1, None, ALU.bitwise_and)
            route(nc.vector.tensor_scalar(tile_ib, pos_i, P.bit_length() - 1, None, ALU.logical_shift_right))
            nc.vector.tensor_copy(slot_of, slot_ib)
            nc.vector.tensor_copy(tile_of, tile_ib).then_inc(s_pos, 1)
            dve.wait_ge(s_pos, 1)
            with dve.Fori(0, NB // 4) as b4:
                for j in range(4):
                    b = b4 * 4 + j
                    dve.wait_ge(s_pm, b + 1)
                    nc.vector.tensor_scalar(slot_oh[j], iota[:, 0:P], slot_of[:, bass.ds(b, 1)],
                                            node_id[:, bass.ds(b, 1)], ALU.is_equal, ALU.mult)
                    nc.vector.tensor_scalar(tile_oh[j], iota[:, 0:NT], tile_of[:, bass.ds(b, 1)], None,
                                            ALU.is_equal).then_inc(s_oh, 1)
            tile0, owner = score.rearrange("p b e -> p (b e)")[:, 0:NT], total.rearrange("p e b -> p (e b)")[:, 0:NT]
            route(nc.vector.tensor_scalar(tile0, iota[:, 0:NT], float(P), None, ALU.mult))
            route(nc.vector.tensor_scalar(owner, tile0, e_start[:, 1:2], None, ALU.is_ge))
            for e in range(2, E):
                route(nc.vector.scalar_tensor_tensor(out=owner, in0=tile0, scalar=e_start[:, e:e + 1], in1=owner,
                                                     op0=ALU.is_ge, op1=ALU.add))
            nc.vector.tensor_scalar(texp_i[:, :, 0], owner, float(HC), None, ALU.mult)
            nc.vector.tensor_scalar(texp_i[:, :, 1], owner, float(C), None, ALU.mult)
            dve.wait_ge(s_pm, 4 + NB + 1)
            node1 = psG[:, 0:NT]
            empty, node = (where.rearrange("p e b -> p (e b)")[:, a * P:a * P + NT] for a in range(2))
            route(nc.vector.tensor_scalar(empty, node1, 1.0, -1.0, ALU.min, ALU.mult))
            route(nc.vector.tensor_scalar(empty, empty, 1.0, None, ALU.add))
            route(nc.vector.scalar_tensor_tensor(out=node, in0=empty, scalar=part1, in1=node1,
                                                 op0=ALU.mult, op1=ALU.add))
            nc.vector.tensor_scalar(perm_i[:, :], node, -1.0, None, ALU.add).then_inc(s_perm, 1)
            dve.wait_ge(s_perm, 1)

            dve.wait_ge(s_bd, 16)
            dve.sem_inc(s_r2free, RING2)

            def row_max(t3, i):
                dve.wait_ge(s_g2[i], t3 * 16 + 16)
                nc.vector.tensor_reduce(negmax[:, i:i + 1], grow[i][:, LOGITS:ROW], AX.X, ALU.max,
                                        negate=True).then_inc(s_n2, 1)

            def routed_tile(t, t3, i, first, last):
                if not last:
                    row_max(t3 + (i + 1) // RING2, (i + 1) % RING2)
                dve.wait_ge(s_e2, t + 1)
                nc.vector.reciprocal(prob[:, i:i + 1], esum[:, i:i + 1]).then_inc(s_d2, 1)
                e256 = dve.value_load(texp_i[0:1, bass.ds(t, 1), 1:2].rearrange("a b c -> a (b c)"),
                                      min_val=0, max_val=(E - 1) * C)
                if not first:
                    dve.wait_ge(s_st[i], t3 * 16)
                nc.vector.tensor_copy(st_out[:, i:i + 1], perm_i[:, bass.ds(t, 1)])
                dve.wait_ge(s_y2, t + 1)
                nc.vector.tensor_tensor(tbuf[i], psY2[i], bd_bc[:, bass.ds(e256, C)], ALU.add).then_inc(s_tl, 1)
                dve.wait_ge(s_tl, t + 1)
                dve.wait_ge(s_d2, t + 1)
                nc.vector.scalar_tensor_tensor(out=ybuf[i], in0=tbuf[i], scalar=prob[:, i:i + 1],
                                               in1=grow[i][:, 0:C], op0=ALU.mult,
                                               op1=ALU.add).then_inc(s_o2, 1)
                dve.wait_ge(s_o2, t + 1)
                dve.sem_inc(s_r2free, 1)

            row_max(0, 0)
            for i in range(RING2):
                routed_tile(i, 0, i, True, False)
            with dve.Fori(1, ROUNDS - 1) as r:
                for i in range(RING2):
                    routed_tile(r * RING2 + i, r, i, False, False)
            for t in range((ROUNDS - 1) * RING2, NT):
                routed_tile(t, t // RING2, t % RING2, False, t == NT - 1)


def kernel(**inputs):
    import numpy as np
    import concourse.bacc as bacc
    from concourse.bass_utils import run_bass_kernel_spmd as run

    def edges(name, fill):
        a = np.ascontiguousarray(inputs[name])
        full = np.full((TABLE * P,), fill, a.dtype)
        full[:EDGES] = a
        return np.ascontiguousarray(full.reshape(TABLE, P).T)

    gate = np.zeros((HID, GATE_COLS), np.float32)
    gate[:, :E] = inputs["L0_ffn_Wg"]
    x = np.zeros((NODES, C), np.float32)
    x[:N] = inputs["x"]
    arrays = {
        "x": x,
        "srcT": edges("src", 0),
        "dstT": edges("dst", N - 1),
        "wT": edges("edge_weight", 0),
        "gnn_WT": np.ascontiguousarray(np.asarray(inputs["L0_gnn_W"]).T),
        "gnn_b": np.ascontiguousarray(inputs["L0_gnn_b"]),
        "W1": np.ascontiguousarray(inputs["L0_ffn_W1"]),
        "b1T": np.ascontiguousarray(np.asarray(inputs["L0_ffn_b1"]).reshape(HC, P).T),
        "Wg": gate,
        "bg": np.ascontiguousarray(inputs["L0_ffn_bg"]),
        "Wd": np.ascontiguousarray(inputs["L0_ffn_Wd"]),
        "bd": np.ascontiguousarray(inputs["L0_ffn_bd"]),
    }
    nc = bacc.Bacc("TRN2", target_bir_lowering=False, num_devices=1)
    feeds, args = {}, []
    for name, a in arrays.items():
        feeds[f"in_{name}"] = a
        args.append(nc.dram_tensor(f"in_{name}", a.shape, mybir.dt.from_np(a.dtype), kind="ExternalInput").ap())
    args.append(nc.dram_tensor("out_0", (N, C), F32, kind="ExternalOutput").ap())
    build(nc, *args)
    r = run(nc, [feeds], core_ids=[0])
    return r.results[0]["out_0"]
```

```python
from contextlib import ExitStack

import concourse.bass as bass
from concourse import mybir

F32 = mybir.dt.float32
I32 = mybir.dt.int32
ALU = mybir.AluOpType
ACT = mybir.ActivationFunctionType
AX = mybir.AxisListType
DVE = mybir.EngineType.DVE
PE = mybir.EngineType.PE

P = 128
N = 12500
C = 256
KC = C // P
HID = 1024
HC = HID // P
E = 8
EPS = 1e-5

GROUP = 512
QB = GROUP // P
NF = -(-N // GROUP)
NODES = NF * GROUP
NB = NODES // P
EDGES = 212500
STEP_TILES = 16
NG = -(-EDGES // (P * STEP_TILES))
SECTIONS = 3
QUAD = 4
QUADS = STEP_TILES // QUAD
NARROW = 64
LANES = 32
TILES = NG * STEP_TILES
TABLE = TILES + STEP_TILES
STEPS = NG + NF

SLOT = GROUP + P
NS = 1 << (2 + -(-STEP_TILES * P // GROUP) - 1).bit_length()
S_RING = 4
ACC0 = STEP_TILES
MM0 = SECTIONS * STEP_TILES
GATE_COLS = LANES
ROW = C + HID + E
LOGITS = C + HID
LN_ROWS = 10
LN_CHUNKS = NB // LN_ROWS
NT = (N + E * (P - 1)) // P
RING2 = 4
ROUNDS = NT // RING2
BATCH = 10
PM0 = 2 * BATCH
IOTA = max(P, STEPS, NB, NT)
PAD_ROW = N + (-N) % 64


RSQRT_MAGIC = float(0x5F3759DF)
RSQRT_LINKS = 13
FFN_LINKS = 8 + RSQRT_LINKS


class Ticker:

    def __init__(self, eng, sem, base, between=None):
        self.eng, self.sem, self.base, self.n, self.between = eng, sem, base, 0, between

    def __call__(self, ins):
        self.n += 1
        ins.then_inc(self.sem, 1)
        if self.between:
            self.between()
        self.eng.wait_ge(self.sem, self.base + self.n)


def build(nc, x, srcT, dstT, wT, gnn_WT, gnn_b, W1, b1T, Wg, bg, Wd, bd, out):
    assert PAD_ROW + P <= NODES and NB % LN_ROWS == 0
    ctx = ExitStack()
    with ctx:
        def sb(name, shape, dt=F32):
            return ctx.enter_context(nc.sbuf_tensor(name, shape, dt))

        def psum(name, shape=(P, 512), dt=F32):
            return ctx.enter_context(nc.psum_tensor(name, list(shape), dt))

        def sem(name):
            return ctx.enter_context(nc.semaphore(name))

        xn_dram = nc.dram_tensor("xn_table", (NODES, C), F32, kind="Internal").ap()
        row_dram = nc.dram_tensor("row_table", (NODES, ROW), F32, kind="Internal").ap()

        big = sb("big", [P, NB * C])
        ln_rows = big[:, :].rearrange("p (r c) -> p r c", c=C)
        xring = big[:, 0:SECTIONS * STEP_TILES * C].rearrange("p (t c) -> p t c", c=C)
        agg0 = SECTIONS * STEP_TILES * C
        agg = big[:, agg0:agg0 + KC * NS * SLOT].rearrange("p (k n) -> p k n", k=KC)
        wd = big[:, 0:E * HC * C].rearrange("p (a c) -> p a c", c=C)
        after_wd = E * HC * C
        bd_bc = big[:, after_wd:after_wd + E * C]
        after_wd = max(after_wd + E * C, agg0 + KC * NS * SLOT)
        assert after_wd + 2 * QB * C + GROUP <= NB * C
        xg, xn2 = (big[:, after_wd + a * QB * C:after_wd + (a + 1) * QB * C].rearrange("p (q c) -> p q c", c=C)
                   for a in range(2))

        gate_parts = big[:, after_wd + 2 * QB * C:after_wd + 2 * QB * C + GROUP]

        src_i = sb("src_i", [P, TABLE], I32)
        w_f = sb("w_f", [P, TABLE])
        rel_f = sb("rel_f", [P, TABLE])
        shift_f = sb("shift_f", [P, TILES // QUAD])
        off_i = sb("off_i", [1, TILES], I32)
        quads_i = sb("quads_i", [1, NG, 2 + QUADS], I32)
        steps_i = sb("steps_i", [P, STEPS, 5], I32)
        stage = sb("stage", [P, SECTIONS, STEP_TILES], I32)
        parts = sb("parts", [P, 2, C])
        sel = parts[:, :, :].rearrange("p a b -> p (a b)").rearrange("p (s n) -> p s n", n=P)
        place = sb("place", [P, QUADS, NARROW])
        selv = sb("sel_narrow", [P, SECTIONS * STEP_TILES * LANES])

        wt = sb("wt", [P, KC, C])
        w1 = sb("w1", [P, KC, HID])
        b1 = sb("b1", [P, HC])
        wg = sb("wg", [P, HC, GATE_COLS])
        fold = sb("fold", [P, E])
        gnn_b_bc = sb("gnn_b_bc", [P, C])
        bg_bc = sb("bg_bc", [P, E])

        zero_col = sb("zero_col", [P, KC])
        ident = sb("ident", [P, P])
        ones = sb("ones", [P, P])
        upper = sb("upper", [P, P])
        iota_i = sb("iota_i", [P, IOTA], I32)
        iota = sb("iota", [P, IOTA])
        part_i = sb("part_i", [P, 1], I32)
        part = sb("part", [P, 1])

        hidT = sb("hidT", [P, HC, GROUP])
        rows = sb("rows", [P, QB, ROW])
        aggs = sb("aggs", [P, KC, GROUP])
        xn2T = sb("xn2T", [P, KC, GROUP])
        stats = sb("stats", [P, 2 * LN_ROWS, 6])
        meanvar = sb("meanvar", [P, NB, 2])
        rstd = sb("rstd", [P, NB])
        nhalf = sb("nhalf", [P, LN_ROWS])
        newton = sb("newton", [P, LN_ROWS])
        nmr = sb("nmr", [P, NB])
        logits = sb("logits", [P, NB, E])
        perm_i = rel_f[:, 0:NT].bitcast(I32)
        texp_i = rel_f[:, NT:3 * NT].bitcast(I32).rearrange("p (t a) -> p t a", a=2)

        scr = hidT[:, :, :].rearrange("p a b -> p (a b)")
        scr2 = rows[:, :, :].rearrange("p a b -> p (a b)")
        dst_i = scr[:, 0:TABLE].bitcast(I32)
        base_i = scr[:, TABLE:2 * TABLE].bitcast(I32)
        base_f = scr2[:, 0:TILES]
        rem_i = scr2[0:1, TILES:2 * TILES].bitcast(I32)
        slot_i = scr2[0:1, 2 * TILES:3 * TILES].bitcast(I32)
        slot_f = scr2[:, 2 * TILES:3 * TILES]
        sel_narrow = selv[:, :].rearrange("p (s n) -> p s n", n=LANES)
        step_masks = selv[:, 0:2 * STEPS + 2 * NG]
        span_tile, span_quad = (xn2T[:, a, 0:NG] for a in range(2))
        u = [selv[:, a * STEPS:(a + 1) * STEPS] for a in range(7)]
        onehot = scr[:, 0:E * NB].rearrange("p (e b) -> p e b", e=E)
        score = scr[:, E * NB:2 * E * NB].rearrange("p (b e) -> p b e", e=E)
        incl = scr[:, 2 * E * NB:3 * E * NB].rearrange("p (e b) -> p e b", e=E)
        total = scr[:, 3 * E * NB:4 * E * NB].rearrange("p (e b) -> p e b", e=E)
        where = scr[:, 4 * E * NB:5 * E * NB].rearrange("p (e b) -> p e b", e=E)
        small = xn2T[:, :, :].rearrange("p a b -> p (a b)")
        best, valid, pos, slot_of, tile_of, tmp_b = (small[:, a * P:a * P + NB] for a in range(6))
        e_rank, e_cnt, e_mod, e_pad, e_cum, e_start = (small[:, 6 * P + a * E:6 * P + (a + 1) * E] for a in range(6))
        part1 = small[:, 7 * P:7 * P + 1]
        assert 2 * BATCH * (P + NT) <= QB * ROW and NB % (2 * BATCH) == 0
        slot_oh = scr2[:, 0:2 * BATCH * P].rearrange("p (h b n) -> p h b n", h=2, b=BATCH)
        tile_oh = scr2[:, 2 * BATCH * P:2 * BATCH * (P + NT)].rearrange("p (h b n) -> p h b n", h=2, b=BATCH)
        zero = gate_parts[:, 0:P]
        node_id = gate_parts[:, P:P + NB]

        psA = [psum("psA0"), psum("psA1")]
        psH = [psum("psH0"), psum("psH1")]
        psE = [psum("psE0"), psum("psE1")]
        psG = psum("psG")
        psR = psum("psR")
        psQ = [psR, psG]

        s_ln_load = [sem(f"ln_load{c}") for c in range(LN_CHUNKS)]
        s_ln_stat = sem("ln_stat")
        s_ln_coef = sem("ln_coef")
        s_ln_applied = sem("ln_applied")
        s_xn_stored = sem("xn_stored")
        s_edges = sem("edges_loaded")
        s_src = sem("sources_loaded")
        s_weights = sem("weights_loaded")
        s_pool_c = sem("pool_consts")
        s_tab = sem("tables_dve")
        s_masks = sem("step_masks_ready")
        s_tabs = sem("tables_ready")
        s_onehot = sem("expert_onehot_ready")
        s_pos = sem("positions_ready")
        s_cnt_mm = sem("count_matmul")
        s_staged = sem("staged")
        s_pass = sem("pool_waits_passed")
        s_pass_dve = sem("dve_waits_passed")
        s_gath = [sem(f"gathered{h}") for h in range(SECTIONS)]
        s_sel = sem("sel_ready")
        s_edge_mm = sem("edge_matmul_done")
        s_narrow_eq = sem("narrow_onehots")
        s_narrow = sem("narrow_sels_ready")
        s_parts = sem("quad_parts_ready")
        s_placed = sem("quad_placed")
        s_acc = sem("accumulated")

        s_aggs = sem("aggs_ready")
        s_ffn = sem("ffn_dve")
        s_z = sem("z_done")
        s_xg = sem("xg_loaded")
        s_x2_st = sem("x2_stored")
        s_lg = sem("logits_ready")
        s_xn2 = sem("xn2_ready")
        s_xt = sem("xn2T_transposed")
        s_xtc = sem("xn2T_copied")
        s_h = sem("hidden_matmul_done")
        s_gelu = sem("gelu_done")
        s_tr = sem("hidden_transposed")
        s_ev = sem("hidden_row_copied")
        s_gp = sem("gate_parts_done")
        s_gc = sem("gate_parts_copied")
        s_g = sem("gate_done")
        s_rows = sem("rows_ready")
        s_rows_free = sem("rows_free")
        s_rows_st = sem("rows_stored")

        s_main = sem("main_done")
        s_wd = sem("wd_loaded")
        s_bd = sem("bd_loaded")
        s_rt = sem("route_dve")
        s_rank = sem("rank_matmul")
        s_oh = sem("slot_onehots")
        s_toh = sem("tile_onehots")
        s_pm = sem("perm_matmul")
        s_perm = sem("perm_ready")

        s_r2free = sem("routed_row_free")
        s_st2 = sem("routed_staged")
        s_g2 = [sem(f"routed_gathered{i}") for i in range(RING2)]
        s_t2 = sem("routed_transposed")
        s_c2 = sem("routed_copied")
        s_y2 = sem("routed_product")
        s_o2 = sem("routed_out_ready")
        s_n2 = sem("routed_negmax")
        s_e2 = sem("routed_expsum")
        s_d2 = sem("routed_prob")
        s_tl = sem("routed_product_read")
        s_st = [sem(f"routed_stored{i}") for i in range(RING2)]

        grow = [rows[:, i, :] for i in range(RING2)]
        hT2 = [hidT[:, i * 2:i * 2 + 2, :].rearrange("p a b -> p (a b)").rearrange("p (c s) -> p c s", c=HC)
               for i in range(RING2)]
        ybuf = [xg[:, i, :] for i in range(RING2)]
        tbuf = [xn2[:, i, :] for i in range(RING2)]
        st_in = stage[:, 0, 0:RING2]
        st_out = sb("st_out", [P, RING2], I32)
        negmax = sb("negmax", [P, RING2])
        expv = sb("expv", [P, RING2, E])
        esum = sb("esum", [P, RING2])
        prob = sb("prob", [P, RING2])
        psT2 = [psA, psH, psE, [psG, psR]]
        psY2 = [psT2[i][0][:, 0:C] for i in range(RING2)]

        def load_values(ap, engine, top):
            return nc.values_load_multi_w_load_instructions(ap, engines=(engine,), min_val=0, max_val=top)[1]

        def step_field(load, k, a, b, engine, top):
            return load(steps_i[0:1, bass.ds(k, 1), a:b].rearrange("a b c -> a (b c)"), engine, top)

        def load_columns(ap, engine, top):
            return nc.values_load_multi_w_load_instructions(
                ap, engines=(engine,), min_val=0, max_val=top,
                skip_runtime_bounds_check_because="columns and kinds are worked out within their bounds")[1]

        block = ctx.enter_context(nc.Block())

        @block.sync
        def _(sp):
            xr = x.rearrange("(p r) c -> p r c", p=P)
            for c in range(LN_CHUNKS):
                sp.dma_start(ln_rows[:, c * LN_ROWS:(c + 1) * LN_ROWS, :],
                             xr[:, c * LN_ROWS:(c + 1) * LN_ROWS, :]).then_inc(s_ln_load[c], 16)
            sp.dma_start(src_i[:, :], srcT[:, :]).then_inc(s_src, 16)
            sp.dma_start(dst_i, dstT[:, :]).then_inc(s_edges, 16)
            sp.dma_start(base_i, dstT[0, :].partition_broadcast(P)).then_inc(s_edges, 16)
            xnr = xn_dram.rearrange("(p r) c -> p r c", p=P)
            for c in range(LN_CHUNKS):
                sp.wait_ge(s_ln_applied, (c + 1) * LN_ROWS)
                sp.dma_start(xnr[:, c * LN_ROWS:(c + 1) * LN_ROWS, :],
                             ln_rows[:, c * LN_ROWS:(c + 1) * LN_ROWS, :]).then_inc(s_xn_stored, 16)
            sp.dma_start(w_f[:, :], wT[:, :]).then_inc(s_weights, 16)
            sp.dma_start(wt[:, :, :], gnn_WT.rearrange("(k p) o -> p k o", p=P)).then_inc(s_weights, 16)
            sp.dma_start(w1[:, :, :], W1.rearrange("(k p) h -> p k h", p=P)).then_inc(s_weights, 16)
            sp.dma_start(wg[:, :, :], Wg.rearrange("(c p) e -> p c e", p=P)).then_inc(s_weights, 16)
            sp.dma_start(b1[:, :], b1T[:, :]).then_inc(s_weights, 16)
            sp.dma_start(gnn_b_bc[:, :], gnn_b.partition_broadcast(P)).then_inc(s_weights, 16)
            sp.dma_start(bg_bc[:, :], bg.partition_broadcast(P)).then_inc(s_weights, 16)
            sp.sem_inc(s_rows_free, 1)
            sp.wait_ge(s_xn_stored, 16 * LN_CHUNKS)
            sp.dma_start(xg[:, :, :], x[0:GROUP, :].rearrange("(q p) c -> p q c", p=P)).then_inc(s_xg, 16)

            def store_x2(f):
                sp.wait_ge(s_xn2, f + 1)
                sp.dma_start(row_dram[bass.ds(f * GROUP, GROUP), 0:C].rearrange("(q p) c -> p q c", p=P),
                             xg[:, :, :]).then_inc(s_x2_st, 16)
                sp.wait_ge(s_x2_st, f * 16 + 16)

            def load_x(f):
                sp.dma_start(xg[:, :, :], x[bass.ds(f * GROUP, GROUP), :]
                             .rearrange("(q p) c -> p q c", p=P)).then_inc(s_xg, 16)

            def store_rows(f):
                sp.wait_ge(s_rows, f + 1)
                sp.dma_start(row_dram[bass.ds(f * GROUP, GROUP), C:ROW].rearrange("(q p) c -> p q c", p=P),
                             rows[:, :, C:ROW]).then_inc(s_rows_st, 16)
                sp.wait_ge(s_rows_st, f * 16 + 16)
                sp.sem_inc(s_rows_free, 1)

            store_x2(0)
            load_x(1)
            with sp.Fori(0, NF - 2) as f:
                store_x2(f + 1)
                load_x(f + 2)
                store_rows(f)
            store_x2(NF - 1)
            store_rows(NF - 2)
            store_rows(NF - 1)
            sp.wait_ge(s_main, 1)
            for e in range(E):
                sp.dma_start(wd[:, e * HC:(e + 1) * HC, :],
                             Wd[e].rearrange("(c p) o -> p c o", p=P)).then_inc(s_wd, 16)
            sp.dma_start(bd_bc, bd.rearrange("e c -> (e c)").partition_broadcast(P)).then_inc(s_bd, 16)

        @block.gpsimd
        def _(pool):
            nc.gpsimd.memset(ones[:, :], 1.0).then_inc(s_pool_c, 1)
            nc.gpsimd.iota(iota_i[:, :], [[1, IOTA]], base=0, channel_multiplier=0).then_inc(s_pool_c, 1)
            nc.gpsimd.iota(part_i[:, :], [[0, 1]], base=0, channel_multiplier=1).then_inc(s_pool_c, 1)
            pool.wait_ge(s_pool_c, 3)
            nc.gpsimd.affine_select(out=ident[:, :], in_=ones[:, :], compare_op=ALU.is_equal, fill=0.0,
                                    base=0, pattern=[[-1, P]], channel_multiplier=1).then_inc(s_pool_c, 1)
            nc.gpsimd.affine_select(out=upper[:, :], in_=ones[:, :], compare_op=ALU.is_gt, fill=0.0,
                                    base=0, pattern=[[1, P]], channel_multiplier=-1).then_inc(s_pool_c, 1)
            pool.wait_ge(s_src, 16)
            pool.wait_ge(s_xn_stored, 16 * LN_CHUNKS)
            def stage_indices(g, h, uses):
                if uses is not None:
                    pool.wait_ge(s_gath[h], uses * (STEP_TILES * 16))
                    pool.sem_inc(s_pass, 1)
                nc.gpsimd.tensor_copy(stage[:, h, :],
                                      src_i[:, bass.ds(g * STEP_TILES, STEP_TILES)]).then_inc(s_staged, 1)

            def gather_section(g, h, turn):
                pool.wait_ge(s_edge_mm, g * STEP_TILES + STEP_TILES // 2)
                pool.sem_inc(s_pass, 1)
                pool.wait_ge(s_staged, g + 1)
                pool.sem_inc(s_pass, 1)
                for j in range(STEP_TILES):
                    if j == STEP_TILES // 2:
                        uses = turn + (h + 1) // SECTIONS
                        stage_indices(g + 1, (h + 1) % SECTIONS, None if isinstance(g, int) and g < SECTIONS - 1 else uses)
                        pool.wait_ge(s_edge_mm, g * STEP_TILES + STEP_TILES)
                        pool.sem_inc(s_pass, 1)
                    nc.gpsimd.indirect_dma_start(
                        out=xring[:, h * STEP_TILES + j, :], out_offset=None, in_=xn_dram[:, :],
                        in_offset=bass.IndirectOffsetOnAxis(ap=stage[:, h, j:j + 1], axis=0)
                    ).then_inc(s_gath[h], 16)

            stage_indices(0, 0, None)
            for h in range(SECTIONS):
                gather_section(h, h, 0)
            with pool.Fori(1, NG // SECTIONS) as i:
                for h in range(SECTIONS):
                    gather_section(i * SECTIONS + h, h, i)
            for g in range(NG // SECTIONS * SECTIONS, NG):
                gather_section(g, g % SECTIONS, g // SECTIONS)

            def gather_routed(t, i):
                pool.wait_ge(s_r2free, t + 1)
                pool.sem_inc(s_pass, 1)
                nc.gpsimd.tensor_copy(st_in[:, i:i + 1], perm_i[:, bass.ds(t, 1)]).then_inc(s_st2, 1)
                pool.wait_ge(s_st2, t + 1)
                pool.sem_inc(s_pass, 1)
                nc.gpsimd.indirect_dma_start(
                    out=grow[i], out_offset=None, in_=row_dram[:, :],
                    in_offset=bass.IndirectOffsetOnAxis(ap=st_in[:, i:i + 1], axis=0)).then_inc(s_g2[i], 16)

            def scatter_routed(t, i):
                pool.wait_ge(s_o2, t + 1)
                pool.sem_inc(s_pass, 1)
                nc.gpsimd.indirect_dma_start(
                    out=out[:, :], out_offset=bass.IndirectOffsetOnAxis(ap=st_out[:, i:i + 1], axis=0),
                    in_=ybuf[i], in_offset=None, bounds_check=N - 1, oob_is_err=False).then_inc(s_st[i], 16)

            pool.wait_ge(s_perm, 1)
            pool.wait_ge(s_rows_free, NF + 1)
            for i in range(RING2):
                gather_routed(i, i)
            with pool.Fori(0, ROUNDS - 1) as r:
                for i in range(RING2):
                    gather_routed(r * RING2 + RING2 + i, i)
                    scatter_routed(r * RING2 + i, i)
            for t in range((ROUNDS - 1) * RING2, NT):
                if t + RING2 < NT:
                    gather_routed(t + RING2, t % RING2)
                scatter_routed(t, t % RING2)
            for i in range(RING2):
                pool.wait_ge(s_st[i], 16 * (-(-(NT - i) // RING2)))

        @block.scalar
        def _(act):
            for c in range(LN_CHUNKS):
                act.wait_ge(s_ln_coef, c + 1)
                with act.Fori(0, 2) as r2:
                    for j in range(LN_ROWS // 2):
                        r = bass.ds(r2 * (LN_ROWS // 2) + c * LN_ROWS + j, 1)
                        nc.scalar.activation(ln_rows[:, r, :], ln_rows[:, r, :], ACT.Identity, bias=nmr[:, r],
                                             scale=rstd[:, r]).then_inc(s_ln_applied, 1)
            act.wait_ge(s_weights, 16 * 7)
            def copy_xn2T(f):
                for k in range(KC):
                    act.wait_ge(s_xt, f * KC + k + 1)
                    nc.scalar.activation(xn2T[:, k, :], psH[k][:, :], ACT.Identity).then_inc(s_xtc, 1)

            def hidden(f):
                for c in range(HC):
                    act.wait_ge(s_h, f * HC + c + 1)
                    nc.scalar.activation(hidT[:, c, :], psH[c % 2][:, :], ACT.Gelu,
                                         bias=b1[:, c:c + 1]).then_inc(s_gelu, 1)
                act.wait_ge(s_gp, f + 1)
                nc.scalar.activation(gate_parts[:, :], psG[:, :], ACT.Identity).then_inc(s_gc, 1)

            copy_xn2T(0)
            with act.Fori(0, NF - 1) as f:
                hidden(f)
                copy_xn2T(f + 1)
            hidden(NF - 1)

            def routed_act(t, i):
                for k in range(2):
                    act.wait_ge(s_t2, t * 2 + k + 1)
                    nc.scalar.activation(hT2[i][:, k * 4:k * 4 + 4, :],
                                         psT2[i][k][:, :].rearrange("p (c s) -> p c s", c=4),
                                         ACT.Identity).then_inc(s_c2, 1)
                act.wait_ge(s_n2, t + 1)
                nc.scalar.activation(expv[:, i, :], grow[i][:, LOGITS:ROW], ACT.Exp,
                                     bias=negmax[:, i:i + 1], accum_out=esum[:, i:i + 1]).then_inc(s_e2, 1)

            with act.Fori(0, ROUNDS) as r:
                for i in range(RING2):
                    routed_act(r * RING2 + i, i)
            for t in range(ROUNDS * RING2, NT):
                routed_act(t, t % RING2)

        @block.tensor
        def _(pe):
            pe.sem_inc(s_edge_mm, MM0)
            pe.wait_ge(s_pool_c, 5)
            pe.wait_ge(s_masks, 1)
            nc.tensor.matmul(psG[:, 0:2 * STEPS + 2 * NG], ones[:, :], step_masks,
                             start=True, stop=True).then_inc(s_cnt_mm, 1)
            pe.wait_ge(s_weights, 16 * 7)
            pe.wait_ge(s_tabs, 1)
            def gather_step(g, h):
                pe.wait_ge(s_gath[h], (g + (SECTIONS - h)) * STEP_TILES * 16 // SECTIONS)
                wide, = load_columns(quads_i[0:1, bass.ds(g, 1), 0:1].rearrange("a b c -> a (b c)"), PE, 1)
                with pe.If(wide == 0):
                    def partial(q):
                        pe.wait_ge(s_narrow, g * 2 + q // 2 + 1)
                        for j in range(QUAD):
                            t = h * STEP_TILES + q * QUAD + j
                            mm = nc.tensor.matmul(psQ[q % 2][j * LANES:(j + 1) * LANES, 0:C], sel_narrow[:, t, :],
                                                  xring[:, t, :], start=True, stop=True)
                        mm.then_inc(s_edge_mm, QUAD)

                    def place_quad(q):
                        pe.wait_ge(s_parts, g * QUADS + q + 1)
                        for k in range(KC):
                            mm = nc.tensor.matmul(psE[q % 2][:, k * NARROW:(k + 1) * NARROW],
                                                  parts[:, q % 2, k * P:(k + 1) * P], place[:, q, :],
                                                  start=True, stop=True)
                        mm.then_inc(s_placed, 1)

                    partial(0)
                    for q in range(1, QUADS):
                        partial(q)
                        place_quad(q - 1)
                    place_quad(QUADS - 1)
                with pe.If(wide == 1):
                    for j in range(STEP_TILES):
                        n = g * STEP_TILES + j
                        pe.wait_ge(s_sel, n + 1)
                        pe.wait_ge(s_acc, n + ACC0 - 1)
                        for k in range(KC):
                            mm = nc.tensor.matmul(psE[j % 2][:, k * P:(k + 1) * P],
                                                  xring[:, h * STEP_TILES + j, k * P:(k + 1) * P],
                                                  sel[:, j % S_RING, :], start=True, stop=True)
                        mm.then_inc(s_edge_mm, 1)
                    pe.sem_inc(s_placed, QUADS)

            def messages(f):
                pe.wait_ge(s_aggs, f + 1)
                for q in range(QB):
                    for k in range(KC):
                        mm = nc.tensor.matmul(psA[q // 2][:, (q % 2) * C:(q % 2 + 1) * C],
                                              aggs[:, k, q * P:(q + 1) * P], wt[:, k, :],
                                              start=(k == 0), stop=(k == KC - 1))
                mm.then_inc(s_z, 1)

            def transpose_xn2(f):
                pe.wait_ge(s_xn2, f + 1)
                for k in range(KC):
                    for q in range(QB):
                        mm = nc.tensor.transpose(psH[k][:, q * P:(q + 1) * P],
                                                 xn2[:, q, k * P:(k + 1) * P], ident[:, :])
                    mm.then_inc(s_xt, 1)

            def hidden(f, following=None):
                pe.wait_ge(s_xtc, f * KC + KC)
                for c in range(HC):
                    if c == 3 and following is not None:
                        messages(following)
                    if c >= 2:
                        pe.wait_ge(s_gelu, f * HC + c - 1)
                    for k in range(KC):
                        mm = nc.tensor.matmul(psH[c % 2][:, :], w1[:, k, c * P:(c + 1) * P], xn2T[:, k, :],
                                              start=(k == 0), stop=(k == KC - 1))
                    mm.then_inc(s_h, 1)
                pe.wait_ge(s_gelu, f * HC + HC)
                for c in range(HC):
                    cg = c % 4
                    mm = nc.tensor.matmul(psG[cg * GATE_COLS:(cg + 1) * GATE_COLS, :], wg[:, c, :], hidT[:, c, :],
                                          start=(c < 4), stop=(c >= 4))
                mm.then_inc(s_gp, 1)
                if following is not None:
                    pe.wait_ge(s_xn2, f + 2)
                else:
                    pe.wait_ge(s_ev, f * (2 * QB))
                for i in range(2 * QB):
                    half, q = i // QB, i % QB
                    if i >= 2:
                        pe.wait_ge(s_ev, f * (2 * QB) + i - 1)
                    for j in range(4):
                        mm = nc.tensor.transpose(psA[i % 2][:, j * P:(j + 1) * P],
                                                 hidT[:, 4 * half + j, q * P:(q + 1) * P], ident[:, :])
                    mm.then_inc(s_tr, 1)
                pe.wait_ge(s_gc, f + 1)
                for q in range(QB):
                    mm = nc.tensor.matmul(psE[0][:, q * E:(q + 1) * E], gate_parts[:, q * P:(q + 1) * P],
                                          fold[:, :], start=True, stop=True)
                mm.then_inc(s_g, 1)

            with pe.Fori(0, STEPS) as k:
                kind, n = step_field(load_values, k, 0, 2, PE, NG)
                for h in range(SECTIONS):
                    with pe.If(kind == h):
                        gather_step(n.with_bounds(min_val=0, max_val=NG - 1), h)
                with pe.If(kind == SECTIONS):
                    before = n.with_bounds(min_val=0, max_val=NF - 2)
                    hidden(before, before + 1)
                    transpose_xn2(before + 1)
                with pe.If(kind == SECTIONS + 1):
                    messages(0)
                    transpose_xn2(0)
            hidden(NF - 1)

            pe.wait_ge(s_onehot, 1)
            oh = scr[:, 0:E * NB]
            for h in range(2):
                nc.tensor.matmul(psA[h][:, 0:4 * NB], upper[:, :], oh[:, h * 4 * NB:(h + 1) * 4 * NB],
                                 start=True, stop=True)
                mm = nc.tensor.matmul(psH[h][:, 0:4 * NB], ones[:, :], oh[:, h * 4 * NB:(h + 1) * 4 * NB],
                                      start=True, stop=True)
            mm.then_inc(s_rank, 1)
            pe.wait_ge(s_pos, 1)
            nc.tensor.matmul(psG[:, 0:NT], zero, ones[:, 0:NT], start=True, stop=False).then_inc(s_pm, PM0)
            with pe.Fori(0, NB // (2 * BATCH)) as n:
                for half in range(2):
                    pe.wait_ge(s_toh, n * 2 + half + 1)
                    for j in range(BATCH):
                        pe.wait_ge(s_oh, n * (2 * BATCH) + half * BATCH + j + 1)
                        nc.tensor.matmul(psG[:, 0:NT], slot_oh[:, half, j, :], tile_oh[:, half, j, :], start=False,
                                         stop=False).then_inc(s_pm, 1)
            nc.tensor.matmul(psG[:, 0:NT], zero, ones[:, 0:NT], start=False, stop=True).then_inc(s_pm, 1)

            def transposes(t3, i):
                pe.wait_ge(s_g2[i], t3 * 16 + 16)
                for k in range(2):
                    for j in range(4):
                        c = 4 * k + j
                        mm = nc.tensor.transpose(psT2[i][k][:, j * P:(j + 1) * P],
                                                 grow[i][:, C + c * P:C + (c + 1) * P], ident[:, :])
                    mm.then_inc(s_t2, 1)

            def product(t, i):
                e8 = pe.value_load(texp_i[0:1, bass.ds(t, 1), 0:1].rearrange("a b c -> a (b c)"),
                                   min_val=0, max_val=(E - 1) * HC)
                pe.wait_ge(s_c2, t * 2 + 2)
                for c in range(HC):
                    mm = nc.tensor.matmul(psY2[i], hT2[i][:, c, :], wd[:, bass.ds(e8 + c, 1), :],
                                          start=(c == 0), stop=(c == HC - 1))
                mm.then_inc(s_y2, 1)

            pe.wait_ge(s_perm, 1)
            pe.wait_ge(s_wd, 16 * E)
            transposes(0, 0)
            with pe.Fori(0, ROUNDS - 1) as r:
                for i in range(RING2):
                    transposes(r + (i + 1) // RING2, (i + 1) % RING2)
                    product(r * RING2 + i, i)
            for t in range((ROUNDS - 1) * RING2, NT):
                if t + 1 < NT:
                    transposes((t + 1) // RING2, (t + 1) % RING2)
                product(t, t % RING2)

        @block.vector
        def _(dve):
            def moments(link, mv, stats):
                n = mv.shape[1]
                diff, squares = nhalf[:, 0:n], newton[:, 0:n]
                nc.vector.tensor_tensor(mv[:, :, 0], stats[:, 0:n, 1], stats[:, 0:n, 4], ALU.add)
                nc.vector.tensor_tensor(squares, stats[:, 0:n, 2], stats[:, 0:n, 5], ALU.add)
                link(nc.vector.tensor_tensor(diff, stats[:, 0:n, 1], stats[:, 0:n, 4], ALU.subtract))
                nc.vector.tensor_scalar(mv[:, :, 0], mv[:, :, 0], 0.5, None, ALU.mult)
                link(nc.vector.scalar_tensor_tensor(out=diff, in0=diff, scalar=0.25, in1=diff,
                                                    op0=ALU.mult, op1=ALU.mult))
                link(nc.vector.scalar_tensor_tensor(out=mv[:, :, 1], in0=squares, scalar=1.0 / C, in1=diff,
                                                    op0=ALU.mult, op1=ALU.add))

            def rsqrt(link, y, var):
                n = y.shape[1]
                v, a = nhalf[:, 0:n], newton[:, 0:n]
                link(nc.vector.tensor_scalar(v, var, EPS, None, ALU.add))
                link(nc.vector.tensor_scalar(a.bitcast(I32), v.bitcast(I32), 1, None, ALU.logical_shift_right))
                link(nc.vector.tensor_scalar(y.bitcast(I32), a.bitcast(I32), -1.0, RSQRT_MAGIC, ALU.mult, ALU.add))
                link(nc.vector.tensor_scalar(v, v, -0.5, None, ALU.mult))
                for _ in range(3):
                    link(nc.vector.tensor_tensor(a, y, y, ALU.mult))
                    link(nc.vector.tensor_tensor(a, a, v, ALU.mult))
                    link(nc.vector.scalar_tensor_tensor(out=y, in0=a, scalar=1.5, in1=y, op0=ALU.add, op1=ALU.mult))

            class RowStats:
                def __init__(self):
                    self.row = 0

                def __call__(self):
                    c, j = divmod(self.row, LN_ROWS)
                    if c < LN_CHUNKS and c <= self.last_chunk:
                        if j == 0:
                            dve.wait_ge(s_ln_load[c], 16)
                        nc.vector.bn_stats(stats[:, (c % 2) * LN_ROWS + j, :],
                                           ln_rows[:, self.row, :]).then_inc(s_ln_stat, 1)
                        self.row += 1

            row_stats = RowStats()
            tick = Ticker(dve, s_tab, 0, row_stats)
            for c in range(LN_CHUNKS):
                row_stats.last_chunk = c + 1
                while row_stats.row < (c + 1) * LN_ROWS:
                    row_stats()
                dve.wait_ge(s_ln_stat, (c + 1) * LN_ROWS)
                cs = slice(c * LN_ROWS, (c + 1) * LN_ROWS)
                moments(tick, meanvar[:, cs, :], stats[:, (c % 2) * LN_ROWS:(c % 2 + 1) * LN_ROWS, :])
                rsqrt(tick, rstd[:, cs], meanvar[:, cs, 1])
                nc.vector.scalar_tensor_tensor(out=nmr[:, cs], in0=meanvar[:, cs, 0], scalar=-1.0,
                                               in1=rstd[:, cs], op0=ALU.mult, op1=ALU.mult).then_inc(s_ln_coef, 1)
            dve.wait_ge(s_pool_c, 5)
            dve.wait_ge(s_edges, 32)
            nc.vector.memset(zero_col[:, :], 0.0)
            nc.vector.tensor_copy(iota[:, :], iota_i[:, :])
            nc.vector.tensor_copy(part[:, :], part_i[:, :])
            lane_i = newton[:, 0:1].bitcast(I32)
            tick(nc.vector.tensor_scalar(lane_i, part_i[:, :], GATE_COLS - 1, None, ALU.bitwise_and))
            tick(nc.vector.tensor_copy(nhalf[:, 0:1], lane_i))
            nc.vector.tensor_scalar(fold[:, :], iota[:, 0:E], nhalf[:, 0:1], None, ALU.is_equal)
            base_q = base_i[:, 0:TILES].rearrange("p (q j) -> p q j", j=QUAD)
            for j in range(QUAD):
                rows_j = slice(j * LANES, (j + 1) * LANES)
                o = nc.vector.tensor_tensor(shift_f[rows_j, :], base_q[rows_j, :, j], base_q[rows_j, :, 0],
                                            ALU.subtract)
            tick(o)
            nc.vector.tensor_scalar(shift_f[:, :], shift_f[:, :], nhalf[:, 0:1], None, ALU.add)
            tick(nc.vector.tensor_tensor(rel_f[:, :], dst_i, base_i, ALU.subtract))
            last_lane = newton[:, 1:2]
            nc.vector.tensor_scalar(last_lane, part[:, :], float(P - 1), None, ALU.is_equal)
            nc.vector.tensor_reduce(span_tile, rel_f[:, 0:TILES].rearrange("p (g t) -> p g t", t=STEP_TILES), AX.X,
                                    ALU.max)
            tick(nc.vector.tensor_tensor(slot_f[:, 0:TILES // QUAD],
                                         dst_i[:, 0:TILES].rearrange("p (q j) -> p q j", j=QUAD)[:, :, QUAD - 1],
                                         base_q[:, :, 0], ALU.subtract))
            tick(nc.vector.tensor_reduce(span_quad, slot_f[:, 0:TILES // QUAD].rearrange("p (g q) -> p g q", q=QUADS),
                                         AX.X, ALU.max))
            for a, span in enumerate((span_tile, span_quad)):
                nc.vector.tensor_scalar(step_masks[:, 2 * STEPS + a * NG:2 * STEPS + (a + 1) * NG], span,
                                        last_lane, None, ALU.mult)
            tick(nc.vector.tensor_copy(base_f, base_i[:, 0:TILES]))
            tick(nc.vector.tensor_scalar(stats[:, 0, 0:1], part[:, :], float(GROUP), float(GROUP),
                                         ALU.mult, ALU.add))
            tick(nc.vector.tensor_scalar(slot_f, base_f, stats[:, 0, 0:1], 0.0, ALU.is_lt, ALU.add,
                                         accum_out=stats[:, 1, 0:1]))
            steps_of = stats[:, 2, 0:1].bitcast(I32)
            tick(nc.vector.tensor_scalar(steps_of, stats[:, 1, 0:1], float(STEP_TILES - 1), None, ALU.add))
            tick(nc.vector.tensor_scalar(steps_of, steps_of, STEP_TILES.bit_length() - 1, None,
                                         ALU.logical_shift_right))
            tick(nc.vector.tensor_tensor(stats[:, 4, 0:1], steps_of, part[:, :], ALU.add))
            nc.vector.tensor_scalar(step_masks[:, 0:STEPS], iota[:, 0:STEPS], stats[:, 4, 0:1], None, ALU.is_equal)
            nc.vector.tensor_scalar(step_masks[:, STEPS:2 * STEPS], iota[:, 0:STEPS], stats[:, 4, 0:1], None,
                                    ALU.is_gt).then_inc(s_masks, 1)
            log_group = GROUP.bit_length() - 1
            nc.vector.tensor_scalar(rem_i, base_i[0:1, 0:TILES], GROUP - 1, None, ALU.bitwise_and)
            tick(nc.vector.tensor_scalar(slot_i, base_i[0:1, 0:TILES], log_group, NS - 1, ALU.logical_shift_right,
                                         ALU.bitwise_and))
            tick(nc.vector.scalar_tensor_tensor(out=off_i[0:1, :], in0=slot_i, scalar=float(SLOT),
                                                in1=rem_i, op0=ALU.mult, op1=ALU.add))
            spans = [psG[0:1, 2 * STEPS + a * NG:2 * STEPS + (a + 1) * NG] for a in range(2)]
            dve.wait_ge(s_cnt_mm, 1)
            nc.vector.tensor_scalar(span_tile[0:1, :], spans[0], float(LANES), None, ALU.is_ge)
            tick(nc.vector.tensor_scalar(span_quad[0:1, :], spans[1], float(NARROW), None, ALU.is_ge))
            nc.vector.tensor_tensor(quads_i[0:1, :, 0], span_tile[0:1, :], span_quad[0:1, :], ALU.max)
            nc.vector.tensor_copy(quads_i[0:1, :, 1:1 + QUADS],
                                  off_i[0:1, :].rearrange("p (g q j) -> p g q j", q=QUADS, j=QUAD)[:, :, :, 0])
            next_i, third = quads_i[0:1, :, 1 + QUADS], span_tile[0:1, :].bitcast(I32)
            tick(nc.vector.tensor_scalar(next_i, iota_i[0:1, 0:NG], 1.0, None, ALU.add))
            tick(nc.vector.tensor_scalar(third, next_i, 171.0, None, ALU.mult))
            tick(nc.vector.tensor_scalar(third, third, 9, None, ALU.logical_shift_right))
            tick(nc.vector.scalar_tensor_tensor(out=next_i, in0=third, scalar=-float(SECTIONS), in1=next_i,
                                                op0=ALU.mult, op1=ALU.add))
            nc.vector.tensor_scalar(next_i, next_i, float(STEP_TILES * LANES), None, ALU.mult)
            nc.vector.tensor_copy(u[2].bitcast(I32), psG[:, 0:STEPS])
            tick(nc.vector.tensor_copy(u[3].bitcast(I32), psG[:, STEPS:2 * STEPS]))
            is_group, groups, gathers, section, prev = (a.bitcast(I32) for a in (u[2], u[3], u[4], u[5], u[0]))
            nc.vector.tensor_scalar(prev, groups, float(NS - 1), None, ALU.add)
            tick(nc.vector.tensor_tensor(gathers, iota_i[:, 0:STEPS], groups, ALU.subtract))
            nc.vector.tensor_scalar(prev, prev, NS - 1, None, ALU.bitwise_and)
            tick(nc.vector.tensor_scalar(section, gathers, 171.0, None, ALU.mult))
            tick(nc.vector.tensor_scalar(section, section, 9, None, ALU.logical_shift_right))
            tick(nc.vector.scalar_tensor_tensor(out=section, in0=section, scalar=-float(SECTIONS), in1=gathers,
                                                op0=ALU.mult, op1=ALU.add))
            is_first, earlier = u[1].bitcast(I32), u[6].bitcast(I32)
            tick(nc.vector.tensor_scalar(is_first, groups, 0.0, None, ALU.is_equal))
            tick(nc.vector.tensor_tensor(is_first, is_first, is_group, ALU.mult))
            tick(nc.vector.scalar_tensor_tensor(out=section, in0=is_group, scalar=float(SECTIONS), in1=section,
                                                op0=ALU.mult, op1=ALU.max))
            nc.vector.tensor_tensor(steps_i[:, :, 0], section, is_first, ALU.add)
            tick(nc.vector.tensor_scalar(earlier, groups, -1.0, 0.0, ALU.add, ALU.max))
            tick(nc.vector.tensor_tensor(earlier, gathers, earlier, ALU.subtract))
            tick(nc.vector.tensor_tensor(earlier, earlier, is_group, ALU.mult))
            nc.vector.tensor_tensor(steps_i[:, :, 1], gathers, earlier, ALU.subtract)
            nc.vector.tensor_copy(steps_i[:, :, 2], gathers)
            slots = is_first
            tick(nc.vector.tensor_scalar(slots, groups, NS - 1, None, ALU.bitwise_and))
            nc.vector.tensor_scalar(steps_i[:, :, 3], slots, float(SLOT), None, ALU.mult)
            tick(nc.vector.tensor_scalar(steps_i[:, :, 4], prev, float(SLOT), float(GROUP), ALU.mult, ALU.add))
            dve.wait_ge(s_weights, 16 * 7)

            def narrow_onehots(g, start, half):
                n = STEP_TILES // 2
                nc.vector.tensor_tensor(
                    selv[:, bass.ds(start + half * n * LANES, n * LANES)].rearrange("p (t n) -> p t n", n=LANES),
                    iota[:, 0:LANES].unsqueeze(1).to_broadcast([P, n, LANES]),
                    rel_f[:, bass.ds(g * STEP_TILES + half * n, n)].unsqueeze(2).to_broadcast([P, n, LANES]),
                    ALU.is_equal).then_inc(s_narrow_eq, 1)

            def narrow_weights(g, start, half):
                n = STEP_TILES // 2
                both = selv[:, bass.ds(start + half * n * LANES, n * LANES)].rearrange("p (t n) -> p t n", n=LANES)
                dve.wait_ge(s_narrow_eq, g * 2 + half + 1)
                nc.vector.tensor_tensor(
                    both, both,
                    w_f[:, bass.ds(g * STEP_TILES + half * n, n)].unsqueeze(2).to_broadcast([P, n, LANES]),
                    ALU.mult).then_inc(s_narrow, 1)

            for half in range(2):
                narrow_onehots(0, 0, half)
            for half in range(2):
                narrow_weights(0, 0, half)
            dve.wait_ge(s_xn_stored, 16 * LN_CHUNKS)
            nc.vector.memset(agg, 0.0).then_inc(s_acc, ACC0)
            dve.wait_ge(s_acc, ACC0)
            nc.vector.memset(stats[:, :, :], 0.0).then_inc(s_tabs, 1)

            def make_sel(g, j):
                col = g * STEP_TILES + j
                nc.vector.tensor_scalar(sel[:, j % S_RING, :], iota[:, 0:P], rel_f[:, bass.ds(col, 1)],
                                        w_f[:, bass.ds(col, 1)], ALU.is_equal, ALU.mult).then_inc(s_sel, 1)

            def gather_step(g):
                wide, *at, start = load_columns(quads_i[0:1, bass.ds(g, 1), :].rearrange("a b c -> a (b c)"), DVE,
                                        (NS - 1) * SLOT + GROUP - 1)
                start = start.with_bounds(min_val=0, max_val=(SECTIONS - 1) * STEP_TILES * LANES)
                with dve.If(wide == 0):
                    def copy_parts(q):
                        dve.wait_ge(s_edge_mm, g * STEP_TILES + (q + 1) * QUAD + MM0)
                        nc.vector.tensor_copy(parts[:, q % 2, :], psQ[q % 2][:, 0:C]).then_inc(s_parts, 1)

                    def accumulate(q):
                        dve.wait_ge(s_placed, g * QUADS + q + 1)
                        dve.wait_ge(s_acc, g * STEP_TILES + q * QUAD + ACC0)
                        win = agg[:, :, bass.ds(at[q], NARROW)]
                        nc.vector.tensor_tensor(win, psE[q % 2][:, 0:KC * NARROW].rearrange("p (k n) -> p k n", k=KC),
                                                win, ALU.add).then_inc(s_acc, QUAD)

                    nc.vector.tensor_tensor(
                        place[:, :, :], iota[:, 0:NARROW].unsqueeze(1).to_broadcast([P, QUADS, NARROW]),
                        shift_f[:, bass.ds(g * QUADS, QUADS)].unsqueeze(2).to_broadcast([P, QUADS, NARROW]),
                        ALU.is_equal)
                    copy_parts(0)
                    narrow_onehots(g + 1, start, 0)
                    copy_parts(1)
                    narrow_weights(g + 1, start, 0)
                    accumulate(0)
                    copy_parts(2)
                    narrow_onehots(g + 1, start, 1)
                    accumulate(1)
                    copy_parts(3)
                    narrow_weights(g + 1, start, 1)
                    accumulate(2)
                    accumulate(3)
                    dve.sem_inc(s_sel, STEP_TILES)
                with dve.If(wide == 1):
                    offs = load_columns(off_i[0:1, bass.ds(g * STEP_TILES, STEP_TILES)], DVE,
                                       (NS - 1) * SLOT + GROUP - 1)
                    for j in range(S_RING // 2):
                        make_sel(g, j)
                    for j in range(STEP_TILES):
                        if j + S_RING // 2 < STEP_TILES:
                            make_sel(g, j + S_RING // 2)
                        n = g * STEP_TILES + j
                        dve.wait_ge(s_edge_mm, n + 1 + MM0)
                        dve.wait_ge(s_acc, n + ACC0)
                        win = agg[:, :, bass.ds(offs[j], P)]
                        nc.vector.tensor_tensor(win, psE[j % 2][:, 0:KC * P].rearrange("p (k n) -> p k n", k=KC),
                                                win, ALU.add).then_inc(s_acc, 1)
                    dve.sem_inc(s_parts, QUADS)
                    for half in range(2):
                        narrow_onehots(g + 1, start, half)
                        narrow_weights(g + 1, start, half)

            def first_part(f, g, slot, spill):
                dve.wait_ge(s_acc, g * STEP_TILES + ACC0)
                dve.sem_inc(s_pass_dve, 1)
                link = Ticker(dve, s_ffn, f * FFN_LINKS)
                here, before = agg[:, :, bass.ds(slot, GROUP)], agg[:, :, bass.ds(spill, P)]
                link(nc.vector.tensor_copy(aggs[:, :, :], here))
                nc.vector.tensor_tensor(aggs[:, :, 0:P], aggs[:, :, 0:P], before, ALU.add).then_inc(s_aggs, 1)
                dve.wait_ge(s_aggs, f + 1)
                nc.vector.tensor_scalar(here, zero_col[:, :].unsqueeze(2).to_broadcast([P, KC, GROUP]), 0.0, None,
                                        ALU.add)
                link(nc.vector.tensor_scalar(before, zero_col[:, :].unsqueeze(2).to_broadcast([P, KC, P]), 0.0,
                                             None, ALU.add))
                dve.wait_ge(s_z, f + 1)
                dve.wait_ge(s_xg, f * 16 + 16)
                x2 = xg[:, :, :]
                for a in range(2):
                    o = nc.vector.tensor_tensor(x2[:, 2 * a:2 * a + 2, :],
                                                psA[a][:, :].rearrange("p (q c) -> p q c", c=C),
                                                x2[:, 2 * a:2 * a + 2, :], ALU.add)
                link(o)
                link(nc.vector.tensor_tensor(x2, x2, gnn_b_bc[:, :].unsqueeze(1).to_broadcast([P, QB, C]), ALU.add))
                for q in range(QB):
                    o = nc.vector.bn_stats(stats[:, q, :], x2[:, q, :])
                link(o)
                moments(link, meanvar[:, 0:QB, :], stats)
                rsqrt(link, rstd[:, 0:QB], meanvar[:, 0:QB, 1])
                for q in range(QB):
                    o = nc.vector.tensor_scalar(xn2[:, q, :], x2[:, q, :], meanvar[:, q, 0:1],
                                                rstd[:, q:q + 1], ALU.subtract, ALU.mult)
                o.then_inc(s_xn2, 1)
                assert link.n == FFN_LINKS, link.n

            def second_part(f):
                dve.wait_ge(s_rows_free, f + 1)
                dve.sem_inc(s_pass_dve, 1)
                for i in range(2 * QB):
                    half, q = i // QB, i % QB
                    dve.wait_ge(s_tr, f * (2 * QB) + i + 1)
                    nc.vector.tensor_copy(rows[:, q, C + half * 512:C + (half + 1) * 512],
                                          psA[i % 2][:, :]).then_inc(s_ev, 1)
                dve.wait_ge(s_g, f + 1)
                lg = rows[:, :, LOGITS:ROW]
                nc.vector.tensor_tensor(lg, psE[0][:, 0:QB * E].rearrange("p (q e) -> p q e", e=E),
                                        bg_bc[:, :].unsqueeze(1).to_broadcast([P, QB, E]), ALU.add
                                        ).then_inc(s_lg, 1)
                dve.wait_ge(s_lg, f + 1)
                dve.wait_ge(s_ev, f * (2 * QB) + 2 * QB)
                dve.sem_inc(s_pass_dve, 1)
                nc.vector.tensor_copy(logits[:, bass.ds(f * QB, QB), :], lg).then_inc(s_rows, 1)

            with dve.Fori(0, STEPS) as k:
                kind, n = step_field(load_values, k, 0, 2, DVE, NG)
                with dve.If(kind == SECTIONS):
                    g, = step_field(load_values, k, 2, 3, DVE, NG)
                    slot, spill = step_field(load_columns, k, 3, 5, DVE, NS * SLOT)
                    before = n.with_bounds(min_val=0, max_val=NF - 2)
                    slot = slot.with_bounds(min_val=0, max_val=(NS - 1) * SLOT)
                    spill = spill.with_bounds(min_val=0, max_val=(NS - 1) * SLOT + GROUP)
                    first_part(before + 1, g, slot, spill)
                    second_part(before)
                with dve.If(kind == SECTIONS + 1):
                    g, = step_field(load_values, k, 2, 3, DVE, NG)
                    first_part(0, g, 0, (NS - 1) * SLOT + GROUP)
                with dve.If(kind < SECTIONS):
                    gather_step(n.with_bounds(min_val=0, max_val=NG - 1))
            second_part(NF - 1)
            dve.wait_ge(s_acc, TILES + ACC0)
            dve.wait_ge(s_rows, NF)
            dve.wait_ge(s_gelu, NF * HC)
            dve.sem_inc(s_main, 1)

            route = Ticker(dve, s_rt, 0)
            nc.vector.memset(zero, 0.0)
            nc.vector.tensor_scalar(e_rank, iota[:, 0:E], -1.0, float(E), ALU.mult, ALU.add)
            nc.vector.tensor_scalar(tmp_b, iota[:, 0:NB], float(P), part[:, 0:1], ALU.mult, ALU.add)
            nc.vector.tensor_scalar(part1, part[:, :], float(PAD_ROW + 1), None, ALU.add)
            route(nc.vector.tensor_reduce(best, logits[:, :, :], AX.X, ALU.max))
            nc.vector.tensor_scalar(valid, tmp_b, float(N), None, ALU.is_lt)
            nc.vector.tensor_scalar(node_id, tmp_b, 1.0, None, ALU.add)
            route(nc.vector.tensor_tensor(score, logits[:, :, :], best.unsqueeze(2).to_broadcast([P, NB, E]),
                                          ALU.is_equal))
            route(nc.vector.tensor_tensor(score, score, e_rank.unsqueeze(1).to_broadcast([P, NB, E]), ALU.mult))
            route(nc.vector.tensor_reduce(best, score, AX.X, ALU.max))
            route(nc.vector.tensor_copy(total, e_rank.unsqueeze(2).to_broadcast([P, E, NB])))
            route(nc.vector.tensor_tensor(onehot, total, best.unsqueeze(1).to_broadcast([P, E, NB]), ALU.is_equal))
            nc.vector.tensor_tensor(onehot, onehot, valid.unsqueeze(1).to_broadcast([P, E, NB]),
                                    ALU.mult).then_inc(s_onehot, 1)
            dve.wait_ge(s_rank, 1)
            for h in range(2):
                o = nc.vector.tensor_copy(scr[:, 3 * E * NB + h * 4 * NB:3 * E * NB + (h + 1) * 4 * NB],
                                          psH[h][:, 0:4 * NB])
            route(o)
            for e in range(E):
                o = nc.vector.tensor_tensor_scan(incl[:, e, :], ones[:, 0:NB], total[:, e, :], 0.0,
                                                 ALU.mult, ALU.add)
            route(o)
            e_int = e_mod.bitcast(I32)
            route(nc.vector.tensor_scalar(e_int, incl[:, :, NB - 1], float(P - 1), None, ALU.add))
            route(nc.vector.tensor_scalar(e_int, e_int, ~(P - 1) & 0xFFFF, None, ALU.bitwise_and))
            route(nc.vector.tensor_copy(e_pad, e_int))
            route(nc.vector.tensor_tensor_scan(e_cum, ones[:, 0:E], e_pad, 0.0, ALU.mult, ALU.add))
            nc.vector.tensor_tensor(e_start, e_cum, e_pad, ALU.subtract)
            route(nc.vector.tensor_tensor(where, incl, total, ALU.subtract))
            for h in range(2):
                part_h = scr[:, 4 * E * NB + h * 4 * NB:4 * E * NB + (h + 1) * 4 * NB]
                o = nc.vector.tensor_tensor(part_h, psA[h][:, 0:4 * NB], part_h, ALU.add)
            route(o)
            route(nc.vector.tensor_tensor(where, where, e_start.unsqueeze(2).to_broadcast([P, E, NB]), ALU.add))
            route(nc.vector.tensor_tensor(where, where, onehot, ALU.mult))
            nc.vector.tensor_scalar(tmp_b, valid, -float(2 * NT * P), float(2 * NT * P), ALU.mult, ALU.add)
            route(nc.vector.tensor_reduce(pos, where.rearrange("p e b -> p b e"), AX.X, ALU.add))
            pos_i, slot_ib, tile_ib = (a.bitcast(I32) for a in (best, valid, tmp_b))
            route(nc.vector.tensor_tensor(pos_i, pos, tmp_b, ALU.add))
            nc.vector.tensor_scalar(slot_ib, pos_i, P - 1, None, ALU.bitwise_and)
            route(nc.vector.tensor_scalar(tile_ib, pos_i, P.bit_length() - 1, None, ALU.logical_shift_right))
            nc.vector.tensor_copy(slot_of, slot_ib)
            nc.vector.tensor_copy(tile_of, tile_ib).then_inc(s_pos, 1)
            dve.wait_ge(s_pos, 1)
            dve.wait_ge(s_rows_free, NF + 1)
            with dve.Fori(0, NB // (2 * BATCH)) as n:
                for half in range(2):
                    dve.wait_ge(s_pm, n * (2 * BATCH) + (half + 1) * BATCH)
                    of = tile_of[:, bass.ds(n * (2 * BATCH) + half * BATCH, BATCH)]
                    nc.vector.tensor_tensor(tile_oh[:, half, :, :],
                                            iota[:, 0:NT].unsqueeze(1).to_broadcast([P, BATCH, NT]),
                                            of.unsqueeze(2).to_broadcast([P, BATCH, NT]),
                                            ALU.is_equal).then_inc(s_toh, 1)
                    for j in range(BATCH):
                        b = n * (2 * BATCH) + half * BATCH + j
                        nc.vector.tensor_scalar(slot_oh[:, half, j, :], iota[:, 0:P], slot_of[:, bass.ds(b, 1)],
                                                node_id[:, bass.ds(b, 1)], ALU.is_equal, ALU.mult).then_inc(s_oh, 1)
            tile0, owner = score.rearrange("p b e -> p (b e)")[:, 0:NT], total.rearrange("p e b -> p (e b)")[:, 0:NT]
            route(nc.vector.tensor_scalar(tile0, iota[:, 0:NT], float(P), None, ALU.mult))
            route(nc.vector.tensor_scalar(owner, tile0, e_start[:, 1:2], None, ALU.is_ge))
            for e in range(2, E):
                route(nc.vector.scalar_tensor_tensor(out=owner, in0=tile0, scalar=e_start[:, e:e + 1], in1=owner,
                                                     op0=ALU.is_ge, op1=ALU.add))
            nc.vector.tensor_scalar(texp_i[:, :, 0], owner, float(HC), None, ALU.mult)
            nc.vector.tensor_scalar(texp_i[:, :, 1], owner, float(C), None, ALU.mult)
            dve.wait_ge(s_pm, PM0 + NB + 1)
            node1 = psG[:, 0:NT]
            empty, node = (where.rearrange("p e b -> p (e b)")[:, a * P:a * P + NT] for a in range(2))
            route(nc.vector.tensor_scalar(empty, node1, 1.0, -1.0, ALU.min, ALU.mult))
            route(nc.vector.tensor_scalar(empty, empty, 1.0, None, ALU.add))
            route(nc.vector.scalar_tensor_tensor(out=node, in0=empty, scalar=part1, in1=node1,
                                                 op0=ALU.mult, op1=ALU.add))
            nc.vector.tensor_scalar(perm_i[:, :], node, -1.0, None, ALU.add).then_inc(s_perm, 1)
            dve.wait_ge(s_perm, 1)

            dve.wait_ge(s_bd, 16)
            dve.sem_inc(s_r2free, RING2)

            def row_max(t3, i):
                dve.wait_ge(s_g2[i], t3 * 16 + 16)
                nc.vector.tensor_reduce(negmax[:, i:i + 1], grow[i][:, LOGITS:ROW], AX.X, ALU.max,
                                        negate=True).then_inc(s_n2, 1)

            def routed_tile(t, t3, i, first, last):
                if not last:
                    row_max(t3 + (i + 1) // RING2, (i + 1) % RING2)
                dve.wait_ge(s_e2, t + 1)
                nc.vector.reciprocal(prob[:, i:i + 1], esum[:, i:i + 1]).then_inc(s_d2, 1)
                e256 = dve.value_load(texp_i[0:1, bass.ds(t, 1), 1:2].rearrange("a b c -> a (b c)"),
                                      min_val=0, max_val=(E - 1) * C)
                if not first:
                    dve.wait_ge(s_st[i], t3 * 16)
                nc.vector.tensor_copy(st_out[:, i:i + 1], perm_i[:, bass.ds(t, 1)])
                dve.wait_ge(s_y2, t + 1)
                nc.vector.tensor_tensor(tbuf[i], psY2[i], bd_bc[:, bass.ds(e256, C)], ALU.add).then_inc(s_tl, 1)
                dve.wait_ge(s_tl, t + 1)
                dve.wait_ge(s_d2, t + 1)
                nc.vector.scalar_tensor_tensor(out=ybuf[i], in0=tbuf[i], scalar=prob[:, i:i + 1],
                                               in1=grow[i][:, 0:C], op0=ALU.mult,
                                               op1=ALU.add).then_inc(s_o2, 1)
                dve.wait_ge(s_o2, t + 1)
                dve.sem_inc(s_r2free, 1)

            row_max(0, 0)
            for i in range(RING2):
                routed_tile(i, 0, i, True, False)
            with dve.Fori(1, ROUNDS - 1) as r:
                for i in range(RING2):
                    routed_tile(r * RING2 + i, r, i, False, False)
            for t in range((ROUNDS - 1) * RING2, NT):
                routed_tile(t, t // RING2, t % RING2, False, t == NT - 1)


def kernel(**inputs):
    import numpy as np
    import concourse.bacc as bacc
    from concourse.bass_utils import run_bass_kernel_spmd as run

    def edges(name, fill):
        a = np.ascontiguousarray(inputs[name])
        full = np.full((TABLE * P,), fill, a.dtype)
        full[:EDGES] = a
        return np.ascontiguousarray(full.reshape(TABLE, P).T)

    gate = np.zeros((HID, GATE_COLS), np.float32)
    gate[:, :E] = inputs["L0_ffn_Wg"]
    x = np.zeros((NODES, C), np.float32)
    x[:N] = inputs["x"]
    arrays = {
        "x": x,
        "srcT": edges("src", 0),
        "dstT": edges("dst", N - 1),
        "wT": edges("edge_weight", 0),
        "gnn_WT": np.ascontiguousarray(np.asarray(inputs["L0_gnn_W"]).T),
        "gnn_b": np.ascontiguousarray(inputs["L0_gnn_b"]),
        "W1": np.ascontiguousarray(inputs["L0_ffn_W1"]),
        "b1T": np.ascontiguousarray(np.asarray(inputs["L0_ffn_b1"]).reshape(HC, P).T),
        "Wg": gate,
        "bg": np.ascontiguousarray(inputs["L0_ffn_bg"]),
        "Wd": np.ascontiguousarray(inputs["L0_ffn_Wd"]),
        "bd": np.ascontiguousarray(inputs["L0_ffn_bd"]),
    }
    nc = bacc.Bacc("TRN2", target_bir_lowering=False, num_devices=1)
    feeds, args = {}, []
    for name, a in arrays.items():
        feeds[f"in_{name}"] = a
        args.append(nc.dram_tensor(f"in_{name}", a.shape, mybir.dt.from_np(a.dtype), kind="ExternalInput").ap())
    args.append(nc.dram_tensor("out_0", (N, C), F32, kind="ExternalOutput").ap())
    build(nc, *args)
    r = run(nc, [feeds], core_ids=[0])
    return r.results[0]["out_0"]
```
